# Optimizing a Trainium2 kernel written in Bass

```python
import numpy as np
import jax
import jax.numpy as jnp

def _softmax(x, axis=-1):
    return jax.nn.softmax(x, axis=axis)
def _gelu(x):
    return jax.nn.gelu(x, approximate=True)
def _silu(x):
    return jax.nn.silu(x)
def _sigmoid(x):
    return jax.nn.sigmoid(x)
def _layernorm(x, axis=-1, eps=1e-5):
    m = jnp.mean(x, axis=axis, keepdims=True)
    v = jnp.var(x, axis=axis, keepdims=True)
    return (x - m) / jnp.sqrt(v + eps)
def _scatter_add(tgt, idx, src, axis=0):
    return tgt.at[idx].add(src)
def _segment_sum(src, seg, n):
    return jax.ops.segment_sum(src, seg, n)

kernel_name = 'mk_adj_resnorm_d4_adj_256_b096fd'

def setup_inputs(seed: int = 0):
    np.random.seed(seed)
    _w = jnp.asarray
    def _rec_inputs():
        import jax
        import jax.numpy as jnp
        _gk = jax.random.key(seed)
        x = -0.0002928 + 1 * jax.random.normal(jax.random.fold_in(_gk, 1), (16, 1024, 256), jnp.float32)
        _a = jax.random.bernoulli(jax.random.fold_in(_gk, 2), 0.015625, (16, 1024, 1024))
        _af = _a.astype(jnp.float32)
        adj = _af
        return x, adj
    x, adj = _rec_inputs()
    def _L0_gnn_setup():
        import jax, jax.numpy as jnp
        import numpy as np
        B, N, D = (4, 4096, 256)
        DENSITY = 32.0 / N
        key = jax.random.key(seed)
        kx, ka, k1, k2, k3, k4 = jax.random.split(key, 6)
        x = jax.random.normal(kx, (B, N, D), dtype=jnp.float32)
        adj = (jax.random.uniform(ka, (B, N, N)) < DENSITY).astype(jnp.float32)
        scale = 0.02
        theta = scale * jax.random.normal(k1, (D, D), dtype=jnp.float32)
        W_h = scale * jax.random.normal(k2, (D, D), dtype=jnp.float32)
        W_t = scale * jax.random.normal(k3, (D, D), dtype=jnp.float32)
        b_t = scale * jax.random.normal(k4, (D,), dtype=jnp.float32)
        return {'x': x, 'adj': adj, 'theta': theta, 'W_h': W_h, 'W_t': W_t, 'b_t': b_t}
    _L0_gnn_all = _L0_gnn_setup()
    _L0_gnn_in = {k: v for k, v in _L0_gnn_all.items() if k in ('theta', 'W_h', 'W_t', 'b_t', )}
    del _L0_gnn_all

    def _L1_gnn_setup():
        import jax, jax.numpy as jnp
        import numpy as np
        K = 4
        EPS = 1e-09
        LEAKY_SLOPE = 0.2
        key = jax.random.key(seed)
        k1, k2, k3, k4, k5 = jax.random.split(key, 5)
        B, N, IN, OUT = (8, 2048, 256, 256)
        h = jax.random.normal(k1, (B, N, IN), dtype=jnp.float32)
        adj = jax.random.uniform(k2, (B, N, N), dtype=jnp.float32)
        W = jax.random.normal(k3, (OUT, IN), dtype=jnp.float32) * 0.05
        conv_w = jax.random.normal(k4, (K,), dtype=jnp.float32)
        conv_b = jax.random.normal(k5, (1,), dtype=jnp.float32)
        return {'h': h, 'adj': adj, 'W': W, 'conv_w': conv_w, 'conv_b': conv_b}
    _L1_gnn_all = _L1_gnn_setup()
    _L1_gnn_in = {k: v for k, v in _L1_gnn_all.items() if k in ('W', 'conv_w', 'conv_b', )}
    del _L1_gnn_all

    def _L2_gnn_setup():
        import jax, jax.numpy as jnp
        import numpy as np
        B, N, D = (4, 4096, 256)
        DENSITY = 0.02
        key = jax.random.key(seed)
        kx, ka1, ka2, kwt, kbt, kwh, kth = jax.random.split(key, 7)
        x = jax.random.normal(kx, (B, N, D), dtype=jnp.float32)
        mask = jax.random.uniform(ka1, (B, N, N)) < DENSITY
        vals = jax.random.uniform(ka2, (B, N, N), dtype=jnp.float32)
        adj = jnp.where(mask, vals, 0.0).astype(jnp.float32)
        s = 0.02
        W_t = s * jax.random.normal(kwt, (D, D), dtype=jnp.float32)
        b_t = s * jax.random.normal(kbt, (D,), dtype=jnp.float32)
        W_h = s * jax.random.normal(kwh, (D, D), dtype=jnp.float32)
        theta = s * jax.random.normal(kth, (D, D), dtype=jnp.float32)
        return {'x': x, 'adj': adj, 'W_t': W_t, 'b_t': b_t, 'W_h': W_h, 'theta': theta}
    _L2_gnn_all = _L2_gnn_setup()
    _L2_gnn_in = {k: v for k, v in _L2_gnn_all.items() if k in ('W_t', 'b_t', 'W_h', 'theta', )}
    del _L2_gnn_all

    def _L3_gnn_setup():
        import jax, jax.numpy as jnp
        import numpy as np
        key = jax.random.key(seed)
        k1, k2, k3, k4 = jax.random.split(key, 4)
        B, N, F_in, F_out = (8, 2048, 256, 256)
        x = jax.random.normal(k1, (B, N, F_in), dtype=jnp.float32)
        adj = jax.random.uniform(k2, (B, N, N), dtype=jnp.float32)
        stdv = 1.0 / np.sqrt(F_out)
        weight = jax.random.uniform(k3, (F_in, F_out), dtype=jnp.float32, minval=-stdv, maxval=stdv)
        bias = jax.random.uniform(k4, (F_out,), dtype=jnp.float32, minval=-stdv, maxval=stdv)
        return {'x': x, 'adj': adj, 'weight': weight, 'bias': bias}
    _L3_gnn_all = _L3_gnn_setup()
    _L3_gnn_in = {k: v for k, v in _L3_gnn_all.items() if k in ('weight', 'bias', )}
    del _L3_gnn_all

    return {
        "x": x,
        "adj": adj,
        "L0_gnn_theta": _L0_gnn_in["theta"],
        "L0_gnn_W_h": _L0_gnn_in["W_h"],
        "L0_gnn_W_t": _L0_gnn_in["W_t"],
        "L0_gnn_b_t": _L0_gnn_in["b_t"],
        "L1_gnn_W": _L1_gnn_in["W"],
        "L1_gnn_conv_w": _L1_gnn_in["conv_w"],
        "L1_gnn_conv_b": _L1_gnn_in["conv_b"],
        "L2_gnn_W_t": _L2_gnn_in["W_t"],
        "L2_gnn_b_t": _L2_gnn_in["b_t"],
        "L2_gnn_W_h": _L2_gnn_in["W_h"],
        "L2_gnn_theta": _L2_gnn_in["theta"],
        "L3_gnn_weight": _L3_gnn_in["weight"],
        "L3_gnn_bias": _L3_gnn_in["bias"],
    }

def reference(x, adj, L0_gnn_theta, L0_gnn_W_h, L0_gnn_W_t, L0_gnn_b_t, L1_gnn_W, L1_gnn_conv_w, L1_gnn_conv_b, L2_gnn_W_t, L2_gnn_b_t, L2_gnn_W_h, L2_gnn_theta, L3_gnn_weight, L3_gnn_bias):
    import jax
    import jax.numpy as jnp
    def _L0_gnn_ref(x, adj, theta, W_h, W_t, b_t):
        import jax, jax.numpy as jnp
        import numpy as np
        B, N, D = (4, 4096, 256)
        DENSITY = 32.0 / N
        in_degrees = jnp.sum(jnp.abs(adj), axis=-1)
        norm = ((in_degrees + 1e-06) ** (-0.5))[..., None]
        f_hom = jnp.einsum('bnd,de->bne', x, theta) * norm
        f_hom = jnp.einsum('bnm,bmd->bnd', adj, f_hom) * norm
        f_het = jnp.einsum('bnd,de->bne', x, W_h)
        gate = jax.nn.sigmoid(jnp.einsum('bnd,de->bne', x, W_t) + b_t)
        out = gate * f_hom + (1.0 - gate) * f_het
        return jax.nn.elu(out)

    def _L1_gnn_ref(h, adj, W, conv_w, conv_b):
        import jax, jax.numpy as jnp
        import numpy as np
        K = 4
        EPS = 1e-09
        LEAKY_SLOPE = 0.2
        h_trans = jnp.einsum('bni,oi->bno', h, W)
        row_sum = adj.sum(axis=2, keepdims=True) + EPS
        adj_norm = adj / row_sum
        curr = h_trans
        out = conv_w[0] * curr
        for k in range(1, K):
            curr = jnp.einsum('bnm,bmo->bno', adj_norm, curr)
            out = out + conv_w[k] * curr
        out = out + conv_b[0]
        return jnp.where(out >= 0, out, LEAKY_SLOPE * out)

    def _L2_gnn_ref(x, adj, W_t, b_t, W_h, theta):
        import jax, jax.numpy as jnp
        import numpy as np
        B, N, D = (4, 4096, 256)
        DENSITY = 0.02
        in_degrees = jnp.sum(adj, axis=-1)
        norm = jnp.power(in_degrees + 1e-06, -0.5)[..., None]
        f_hom = jnp.einsum('bnd,de->bne', x, theta) * norm
        f_hom = jnp.einsum('bnm,bmd->bnd', adj, f_hom) * norm
        f_het = jnp.einsum('bnd,de->bne', x, W_h)
        gate = jax.nn.sigmoid(jnp.einsum('bnd,de->bne', x, W_t) + b_t)
        out = gate * f_hom + (1.0 - gate) * f_het
        return jax.nn.elu(out)

    def _L3_gnn_ref(x, adj, weight, bias):
        import jax, jax.numpy as jnp
        import numpy as np
        support = jnp.einsum('bni,io->bno', x, weight)
        out = jnp.einsum('bnm,bmo->bno', adj, support)
        return out + bias

    x = _layernorm(x + _L0_gnn_ref(x, adj, L0_gnn_theta, L0_gnn_W_h, L0_gnn_W_t, L0_gnn_b_t), axis=-1)
    x = _layernorm(x + _L1_gnn_ref(x, adj, L1_gnn_W, L1_gnn_conv_w, L1_gnn_conv_b), axis=-1)
    x = _layernorm(x + _L2_gnn_ref(x, adj, L2_gnn_W_t, L2_gnn_b_t, L2_gnn_W_h, L2_gnn_theta), axis=-1)
    x = _layernorm(x + _L3_gnn_ref(x, adj, L3_gnn_weight, L3_gnn_bias), axis=-1)
    return x


_drawn_inputs = setup_inputs


def setup_inputs(seed=0):
    import zlib

    import numpy as np

    out = dict(_drawn_inputs(seed))
    spreads = {}
    factors = {'L0_gnn_b_t': 36.304,
     'L2_gnn_b_t': 40.126,
     'L3_gnn_bias': 4.175,
     'L0_gnn_W_t': 2.673,
     'L2_gnn_W_t': 2.729}
    for name, (base, spread) in spreads.items():
        noise = np.random.default_rng([zlib.crc32(name.encode()), seed]).standard_normal(out[name].shape)
        drawn = base * np.exp(spread * noise) if base else spread * noise
        out[name] = jnp.asarray(drawn.astype(out[name].dtype))
    for name, factor in factors.items():
        out[name] = (out[name] * factor).astype(out[name].dtype)
    return out
```

```python
from contextlib import ExitStack

import concourse.bass as bass
from concourse import mybir

F32 = mybir.dt.float32
F32R = mybir.dt.float32r
I32 = mybir.dt.int32
ALU = mybir.AluOpType
ACT = mybir.ActivationFunctionType
AX = mybir.AxisListType

P = 128
SLOTS = 2
LAYERS = 4
GATED = (0, 2)
CHAIN = 1
LAST = 3
LEAKY_SLOPE = 0.2
LN_EPS = 1e-5
DEGREE_EPS = 1e-6
ROW_SUM_EPS = 1e-9
STAGES = 2
PRODUCT_BANKS = 3
SIGN_OR_LOW_BITS = -(1 << 31) + (1 << 12) - 1

STEPS = [(layer, s) for layer in range(LAYERS) for s in range(SLOTS)]
FIRST_MATRIX = (0, 3, 4, 7)
MATRICES = 8
ABS_NORM, NORM, INV_SUM, CONV = 0, 1, 2, 2


def step_of(layer, s):
    return layer * SLOTS + s


def product_of(layer, s):
    return (s, 2 + 3 * s, 8 + s, 10 + s)[layer]


def products_in(layer):
    return 3 if layer == CHAIN else 1


PRODUCTS = [(layer, s, stage) for layer, s in STEPS for stage in range(products_in(layer))]


def gated_step_of(layer, s):
    return GATED.index(layer) * SLOTS + s


class Signal:

    def __init__(self, sem, per_round):
        self.sem, self.per_round = sem, per_round

    def at(self, rnd, n):
        return rnd * self.per_round + (self.per_round + n)


def gnn_stack(nc, x, adj_t, theta0, wh0, wt0, bt0, w1t, conv_w, conv_b, wt2, bt2, wh2, theta2, w3,
              bias3, out):
    B, N, D = x.shape
    T = N // P
    K = D // P
    PAIRS = T // 2
    ROUNDS = B // SLOTS
    TAPS = conv_w.shape[0]
    assert D == 2 * P and T == 8 and TAPS == 4 and B == ROUNDS * SLOTS

    with ExitStack() as ctx:
        def sb(name, shape, dt=F32):
            return ctx.enter_context(nc.sbuf_tensor(name, shape, dt))

        def ps(name, shape):
            return ctx.enter_context(nc.psum_tensor(name, shape, F32))

        def sem(name):
            return ctx.enter_context(nc.semaphore(name))

        def signal(name, per_round):
            return Signal(sem(name), per_round)

        adj = [sb(f"adj{s}", [P, T, N], F32R) for s in range(SLOTS)]
        stage_adj = sb("stage_adj", [P, STAGES, N])
        xs = [sb(f"x{s}", [P, T, D]) for s in range(SLOTS)]
        xt_hi = sb("xt_hi", [P, K, N], F32R)
        xt_lo = sb("xt_lo", [P, K, N], F32R)
        f_hi = sb("f_hi", [P, 2, T, D], F32R)
        f_lo = sb("f_lo", [P, 2, T, D], F32R)
        side = sb("side", [P, T, D])
        gate = sb("gate", [P, T, D])
        w_hi = sb("w_hi", [P, K, MATRICES, D], F32R)
        w_lo = sb("w_lo", [P, K, MATRICES, D], F32R)
        mixed = sb("mixed", [P, 2, 2, D])
        expo = sb("expo", [P, 2, 2, D])
        y = sb("y", [P, 3, 2, D])
        gate_bias = sb("gate_bias", [P, 2, D])
        last_bias = sb("last_bias", [P, D])
        taps = sb("taps", [P, TAPS + 1])
        abs_adj = sb("abs_adj", [P, N])
        seen_bits = abs_adj[:, :].bitcast(I32)
        identity = sb("identity", [P, P])
        ones = sb("ones", [P, 2], F32R)
        minus_half = sb("minus_half", [P, T])
        norms = sb("norms", [P, SLOTS, 6, T])
        sums = sb("sums", [P, SLOTS, T, 2])
        row_bits = sb("row_bits", [P, 1])
        odd_row = sb("odd_row", [P, 1])
        odd_rows = sb("odd_rows", [1, SLOTS], I32)
        stats = sb("stats", [P, 2, 6])
        mean_var = sb("mean_var", [P, T, 2])
        rstd = sb("rstd", [P, T])
        weight_f32 = side[:, :, :].rearrange("p (j k) d -> p j k d", k=K), \
            gate[:, :, :].rearrange("p (j k) d -> p j k d", k=K)

        prod_ps = [ps(f"prod_ps{b}", [P, 2 * D]) for b in range(PRODUCT_BANKS)]
        turn_ps = [ps(f"turn_ps{b}", [P, K, 2 * P]) for b in range(2)]
        x_ps = [ps(f"x_ps{b}", [P, 2 * D]) for b in range(2)]
        misc_ps = ps("misc_ps", [P, 2 * D])
        logit_ps = misc_ps[:, 0:D]
        sums_ps = misc_ps[:, D:D + 2 * T].rearrange("p (t j) -> p t j", j=2)
        count_ps = misc_ps[0:1, D + 2 * T:D + 2 * T + 1]

        load_w = sem("load_w")
        load_x = [sem(f"load_x{s}") for s in range(SLOTS)]
        staged = [sem(f"staged{r}") for r in range(STAGES)]
        moved = [sem(f"moved{r}") for r in range(STAGES)]
        stored = [sem(f"stored{s}") for s in range(SLOTS)]
        identity_steps = sem("identity_steps")
        ones_set = sem("ones_set")
        half_set = sem("half_set")
        w_hi_made = sem("w_hi_made")
        w_lo_made = sem("w_lo_made")
        waits_apart = sem("waits_apart")

        steps, gated_steps = LAYERS * SLOTS, len(GATED) * SLOTS
        products = len(PRODUCTS)
        pe_turned = signal("pe_turned", steps * PAIRS)
        pe_x = signal("pe_x", steps * T)
        pe_prod = signal("pe_prod", products * T)
        pe_flag = signal("pe_flag", SLOTS)
        pe_sums = signal("pe_sums", SLOTS)
        pe_abs_used = signal("pe_abs_used", SLOTS * T)
        act_xt_hi = signal("act_xt_hi", steps * PAIRS)
        act_f_hi = signal("act_f_hi", products * T)
        act_gate = signal("act_gate", gated_steps * T)
        act_relu = signal("act_relu", gated_steps * PAIRS)
        act_exp = signal("act_exp", gated_steps * PAIRS)
        act_abs = signal("act_abs", SLOTS * T)
        dve_bits = signal("dve_bits", SLOTS * (T - 1))
        dve_masked = signal("dve_masked", SLOTS)
        dve_row = signal("dve_row", SLOTS)
        dve_odd_row = signal("dve_odd_row", SLOTS)
        dve_flag = signal("dve_flag", SLOTS)
        dve_sums = signal("dve_sums", SLOTS)
        dve_shifted = signal("dve_shifted", SLOTS)
        dve_inv = signal("dve_inv", SLOTS)
        dve_conv = signal("dve_conv", SLOTS)
        dve_xt = signal("dve_xt", steps * PAIRS)
        dve_logit = signal("dve_logit", gated_steps * T)
        dve_f = signal("dve_f", products * T)
        dve_link = signal("dve_link", 2 * SLOTS * T)
        dve_last = signal("dve_last", steps * T)
        dve_act = signal("dve_act", 3 * SLOTS * PAIRS)
        dve_y = signal("dve_y", 3 * SLOTS * PAIRS)
        dve_stats = signal("dve_stats", steps * PAIRS)
        dve_mean = signal("dve_mean", steps * PAIRS)
        dve_x = signal("dve_x", steps * PAIRS)
        pool_shifted = signal("pool_shifted", 2 * SLOTS)
        pool_norm = signal("pool_norm", SLOTS)
        pool_gate = signal("pool_gate", gated_steps * PAIRS)
        pool_mul = signal("pool_mul", gated_steps * PAIRS)
        pool_pre = signal("pool_pre", gated_steps * PAIRS)
        pool_side = signal("pool_side", SLOTS * PAIRS)
        pool_var = signal("pool_var", steps * PAIRS)
        pool_rstd = signal("pool_rstd", steps * PAIRS)

        x_dram = x.rearrange("(i s) (t p) d -> i s p t d", s=SLOTS, p=P)
        out_dram = out.rearrange("(i s) (t p) d -> i s p t d", s=SLOTS, p=P)
        adj_dram = adj_t.rearrange("(i s) (t p) n -> i s p t n", s=SLOTS, p=P)

        def f_event(layer, s, stage, t):
            return (product_of(layer, s) + stage) * T + t + 1

        def last_event(layer, s, t):
            return step_of(layer, s) * T + t + 1

        def pair_event(layer, s, u):
            return step_of(layer, s) * PAIRS + u + 1

        def gated_event(layer, s, u):
            return gated_step_of(layer, s) * PAIRS + u + 1

        def step_before(layer, s, n=1):
            at = step_of(layer, s) - n
            return (*STEPS[at % len(STEPS)], at // len(STEPS))

        def moves(rnd, s, m):
            return (rnd * SLOTS + s) * (T // STAGES * 16) + (m // STAGES + 1) * 16

        def product_bank(layer, s, stage, t):
            return prod_ps[((product_of(layer, s) + stage) * T + t) % PRODUCT_BANKS][:, 0:D]

        def store(engine, rnd, s):
            wait_apart(engine, dve_x.sem, dve_x.at(rnd, pair_event(LAST, s, PAIRS - 1)))
            engine.dma_start(out_dram[rnd, s], xs[s][:, :, :]).then_inc(stored[s], 16)

        def load_next(engine, rnd, s):
            wait_apart(engine, stored[s], rnd * 16 + 16)
            engine.dma_start(xs[s][:, :, :], x_dram[rnd + 1, s]).then_inc(load_x[s], 16)

        def wait_apart(engine, semaphore, value):
            engine.wait_ge(semaphore, value)
            engine.sem_inc(waits_apart, 1)

        def pair(tile, u):
            return tile[:, 2 * u:2 * u + 2, :]

        block = ctx.enter_context(nc.Block())

        @block.sync
        def _(sp):
            for j, w in enumerate((theta0, wh0, wt0, w1t, theta2, wh2, wt2, w3)):
                sp.dma_start(weight_f32[j // 4][:, j % 4], w.rearrange("(k p) d -> p k d", p=P)).then_inc(load_w, 16)
            for j, b in enumerate((bt0, bt2)):
                sp.dma_start(gate_bias[:, j, :], b.partition_broadcast(P)).then_inc(load_w, 16)
            sp.dma_start(last_bias[:, :], bias3.partition_broadcast(P)).then_inc(load_w, 16)
            sp.dma_start(taps[:, 0:TAPS], conv_w.partition_broadcast(P)).then_inc(load_w, 16)
            sp.dma_start(taps[:, TAPS:TAPS + 1], conv_b.partition_broadcast(P)).then_inc(load_w, 16)
            def stream(rnd, s):
                def stage(m):
                    wait_apart(sp, moved[m % STAGES], moves(rnd, s, m) - 16)
                    sp.dma_start(stage_adj[:, m % STAGES, :], adj_dram[rnd, s, :, m, :]).then_inc(staged[m % STAGES], 16)

                for m in range(STAGES):
                    stage(m)
                yield
                for m in range(T):
                    wait_apart(sp, staged[m % STAGES], moves(rnd, s, m))
                    sp.dma_start(adj[s][:, m, :].bitcast(F32), stage_adj[:, m % STAGES, :]).then_inc(moved[m % STAGES], 16)
                    if m + STAGES < T:
                        stage(m + STAGES)
                    if m == T // 2:
                        yield

            for s in range(SLOTS):
                sp.dma_start(xs[s][:, :, :], x_dram[0, s]).then_inc(load_x[s], 16)
                for _ in stream(0, s):
                    pass
            if ROUNDS > 1:
                with sp.Fori(0, ROUNDS - 1) as rnd:
                    for s in range(SLOTS):
                        loads = stream(rnd + 1, s)
                        next(loads)
                        wait_apart(sp, pe_prod.sem, pe_prod.at(rnd, f_event(LAST, s, 0, T - 1)))
                        next(loads)
                        if s == 1:
                            store(sp, rnd, 1)
                        for _ in loads:
                            pass
                    load_next(sp, rnd, 1)
            store(sp, ROUNDS - 1, 1)
            sp.wait_ge(stored[1], ROUNDS * 16)

        @block.tensor
        def _(pe):
            for sig in (pe_turned, pe_x, pe_prod, pe_flag, pe_sums, pe_abs_used):
                pe.sem_inc(sig.sem, sig.per_round)
            pe.wait_ge(identity_steps, 2)
            pe.wait_ge(ones_set, 1)
            pe.wait_ge(w_lo_made, MATRICES)

            def turn(rnd, layer, s):
                for u in range(PAIRS):
                    n = pair_event(layer, s, u)
                    if layer == 0:
                        if u == 0:
                            pe.wait_ge(load_x[s], rnd * 16 + 16)
                    else:
                        pe.wait_ge(dve_x.sem, dve_x.at(rnd, pair_event(layer - 1, s, u)))
                    pe.wait_ge(dve_xt.sem, dve_xt.at(rnd, n - 2))
                    for t in range(2):
                        for k in range(K):
                            last = nc.tensor.transpose(turn_ps[u % 2][:, k, t * P:(t + 1) * P],
                                                       xs[s][:, 2 * u + t, k * P:(k + 1) * P], identity[:, :])
                    last.then_inc(pe_turned.sem, 1)

            def count_odd_rows(rnd, s):
                pe.wait_ge(dve_odd_row.sem, dve_odd_row.at(rnd, s + 1))
                nc.tensor.matmul(count_ps, odd_row[:, :], odd_row[:, :],
                                 start=True, stop=True).then_inc(pe_flag.sem, 1)

            def sum_rows(rnd, s, general):
                for m in range(T):
                    if general:
                        pe.wait_ge(act_abs.sem, act_abs.at(rnd, s * T + m + 1))
                    for t in range(T):
                        n = slice(t * P, (t + 1) * P)
                        opened = dict(start=(m == 0 and t == 0), stop=(m == T - 1), skip_group_check=True)
                        closed = dict(start=False, stop=(m == T - 1), skip_group_check=True)
                        if general:
                            one = ones[:, 0:1].bitcast(F32)
                            nc.tensor.matmul(sums_ps[:, t, 0:1], abs_adj[:, n], one, **opened)
                            last = nc.tensor.matmul(sums_ps[:, t, 1:2], adj[s][:, m, n].bitcast(F32), one, **closed)
                        else:
                            last = nc.tensor.matmul(sums_ps[:, t, :], adj[s][:, m, n], ones[:, :], **opened)
                    if general:
                        last.then_inc(pe_abs_used.sem, 1)
                        if m == T - 1:
                            pe.wait_ge(pe_abs_used.sem, pe_abs_used.at(rnd, s * T + T))
                            pe.sem_inc(pe_sums.sem, 1)
                if not general:
                    last.then_inc(pe_sums.sem, 1)
                    pe.sem_inc(pe_abs_used.sem, T)

            def through_weights(rnd, layer, s):
                first = FIRST_MATRIX[layer]
                gated = layer in GATED
                for t in range(T):
                    if t % 2 == 0:
                        pe.wait_ge(dve_xt.sem, dve_xt.at(rnd, pair_event(layer, s, t // 2)))
                    if t >= 2:
                        free = f_event(layer, s, 0, t - 2)
                    else:
                        pl, p_s, back = step_before(layer, s)
                        free = f_event(pl, p_s, 0, T + t - 2) + back * products * T
                    pe.wait_ge(dve_f.sem, dve_f.at(rnd, free))
                    tile = slice(t * P, (t + 1) * P)
                    parts = [(x_part, w_part, k) for k in range(K)
                             for x_part, w_part in ((xt_hi, w_hi), (xt_hi, w_lo), (xt_lo, w_hi))]
                    width = 2 if gated else 1
                    for n, (x_part, w_part, k) in enumerate(parts):
                        last = nc.tensor.matmul(x_ps[t % 2][:, 0:width * D], x_part[:, k, tile],
                                                w_part[:, k, first:first + width, :],
                                                start=n == 0, stop=n == len(parts) - 1)
                    if gated:
                        pe.wait_ge(dve_logit.sem, dve_logit.at(rnd, gated_step_of(layer, s) * T + t))
                        if layer == 0 and t == 0:
                            pe.wait_ge(dve_sums.sem, dve_sums.at(rnd, s + 1))
                        for n, (x_part, w_part, k) in enumerate(parts):
                            last = nc.tensor.matmul(logit_ps, x_part[:, k, tile], w_part[:, k, first + 2, :],
                                                    start=n == 0, stop=n == len(parts) - 1)
                    last.then_inc(pe_x.sem, 1)

            def bank_free(rnd, layer, s, stage, t):
                n = (product_of(layer, s) + stage) * T + t - PRODUCT_BANKS
                if n < 0:
                    n, rnd = n + products * T, rnd - 1
                layer, s, stage = PRODUCTS[n // T]
                if stage < products_in(layer) - 1:
                    pe.wait_ge(dve_link.sem, dve_link.at(rnd, (s * 2 + stage) * T + n % T + 1))
                else:
                    pe.wait_ge(dve_last.sem, dve_last.at(rnd, last_event(layer, s, n % T)))

            def product(rnd, layer, s, stage, tiles, general):
                p = product_of(layer, s) + stage
                blocks = [(m, t) for m in range(T) for t in (0, 1) if t in tiles]
                blocks += [(m, t) for t in tiles if t > 1 for m in range(T)]
                for m, t in blocks:
                    if m == 0:
                        bank_free(rnd, layer, s, stage, t)
                    if t == 0:
                        pe.wait_ge(dve_f.sem, dve_f.at(rnd, p * T + m + 1))
                    n = slice(t * P, (t + 1) * P)
                    into = product_bank(layer, s, stage, t)
                    for part in (f_hi, f_lo):
                        f = part[:, p % 2, m, :]
                        block = adj[s][:, m, n]
                        if general:
                            block, f = block.bitcast(F32), f.bitcast(F32)
                        last = nc.tensor.matmul(into, block, f,
                                                start=(m == 0 and part is f_hi),
                                                stop=(m == T - 1 and part is f_lo))
                    if m == T - 1:
                        last.then_inc(pe_prod.sem, 1)

            def flag_of(rnd, s):
                wait_apart(pe, dve_flag.sem, dve_flag.at(rnd, s + 1))
                return pe.value_load(odd_rows[0:1, s:s + 1])

            with pe.Fori(0, ROUNDS) as rnd:
                odd = [None] * SLOTS

                def find_sums(s):
                    odd[s] = flag_of(rnd, s)
                    with pe.If(odd[s]):
                        sum_rows(rnd, s, True)
                    with pe.Else():
                        sum_rows(rnd, s, False)

                turn(rnd, 0, 0)
                count_odd_rows(rnd, 0)
                find_sums(0)
                for layer, s in STEPS:
                    through_weights(rnd, layer, s)
                    for stage in range(products_in(layer)):
                        last_stage = stage == products_in(layer) - 1
                        for half in range(2):
                            tiles = range(half * T // 2, (half + 1) * T // 2)
                            with pe.If(odd[s]):
                                product(rnd, layer, s, stage, tiles, True)
                            with pe.Else():
                                product(rnd, layer, s, stage, tiles, False)
                            if last_stage and half == 0 and (layer, s) != STEPS[-1]:
                                turn(rnd, *STEPS[step_of(layer, s) + 1])
                                if (layer, s) == (0, 0):
                                    count_odd_rows(rnd, 1)
                                    find_sums(1)

        @block.scalar
        def _(act):
            for sig in (act_xt_hi, act_f_hi, act_gate, act_relu, act_exp, act_abs):
                act.sem_inc(sig.sem, sig.per_round)
            act.wait_ge(load_w, 16 * (MATRICES + 5))
            for j in range(MATRICES):
                nc.scalar.activation(w_hi[:, :, j, :], weight_f32[j // 4][:, j % 4], ACT.Copy).then_inc(w_hi_made, 1)
            act.wait_ge(w_lo_made, MATRICES)

            def turned(rnd, layer, s):
                for u in range(PAIRS):
                    act.wait_ge(pe_turned.sem, pe_turned.at(rnd, pair_event(layer, s, u)))
                    nc.scalar.activation(xt_hi[:, :, 2 * u * P:(2 * u + 2) * P], turn_ps[u % 2][:, :, :],
                                         ACT.Copy).then_inc(act_xt_hi.sem, 1)

            def absolute(rnd, s):
                wait_apart(act, dve_flag.sem, dve_flag.at(rnd, s + 1))
                odd = act.value_load(odd_rows[0:1, s:s + 1])
                with act.If(odd):
                    for m in range(T):
                        act.wait_ge(pe_abs_used.sem, pe_abs_used.at(rnd, s * T + m))
                        nc.scalar.activation(abs_adj[:, :], adj[s][:, m, :].bitcast(F32), ACT.Abs).then_inc(act_abs.sem, 1)
                with act.Else():
                    act.sem_inc(act_abs.sem, T)

            def tanh(rnd, layer, s, t):
                n = gated_step_of(layer, s) * T + t + 1
                act.wait_ge(dve_logit.sem, dve_logit.at(rnd, n))
                nc.scalar.activation(gate[:, t, :], gate[:, t, :], ACT.Tanh, scale=0.5).then_inc(act_gate.sem, 1)

            def exponential(rnd, layer, s, u):
                n = gated_event(layer, s, u)
                act.wait_ge(pool_pre.sem, pool_pre.at(rnd, n))
                nc.scalar.activation(expo[:, u % 2], mixed[:, u % 2], ACT.Relu, scale=-1.0).then_inc(act_relu.sem, 1)
                act.wait_ge(act_relu.sem, act_relu.at(rnd, n))
                nc.scalar.activation(expo[:, u % 2], expo[:, u % 2], ACT.Exp, scale=-1.0).then_inc(act_exp.sem, 1)

            def one_round(rnd, more):
                turned(rnd, 0, 0)
                absolute(rnd, 0)
                for layer, s in STEPS:
                    gated = layer in GATED
                    before, before_s, back = step_before(layer, s)
                    if layer == 0:
                        act.wait_ge(pool_norm.sem, pool_norm.at(rnd, s + 1))
                    for t in range(T):
                        act.wait_ge(pe_x.sem, pe_x.at(rnd, step_of(layer, s) * T + t + 1))
                        if gated:
                            if before in GATED:
                                act.wait_ge(pool_pre.sem, pool_pre.at(rnd, gated_event(before, before_s, t // 2)))
                            elif before == CHAIN:
                                act.wait_ge(dve_act.sem, dve_act.at(rnd, step_of(before, before_s) * PAIRS + t // 2 + 1))
                            else:
                                act.wait_ge(dve_last.sem, dve_last.at(rnd + back, last_event(before, before_s, t)))
                            nc.scalar.activation(side[:, t, :], x_ps[t % 2][:, D:2 * D], ACT.Copy)
                            norm = norms[:, s, ABS_NORM if layer == 0 else NORM, t:t + 1]
                        else:
                            norm = 1.0
                        nc.scalar.activation(f_hi[:, product_of(layer, s) % 2, t, :], x_ps[t % 2][:, 0:D],
                                             ACT.Copy, scale=norm).then_inc(act_f_hi.sem, 1)
                        if gated and t >= 1:
                            tanh(rnd, layer, s, t - 1)
                        if before in GATED and t == 1 and (layer, s) != (0, 0):
                            exponential(rnd, before, before_s, PAIRS - 1)
                    if gated:
                        tanh(rnd, layer, s, T - 1)
                    if (layer, s) == STEPS[-1]:
                        store(act, rnd, 0)
                        if more:
                            load_next(act, rnd, 0)
                    for stage in range(products_in(layer)):
                        p = product_of(layer, s) + stage
                        last_stage = stage == products_in(layer) - 1
                        for t in range(T):
                            if not last_stage:
                                act.wait_ge(pe_prod.sem, pe_prod.at(rnd, p * T + t + 1))
                                nc.scalar.activation(f_hi[:, (p + 1) % 2, t, :], product_bank(layer, s, stage, t),
                                                     ACT.Copy, scale=norms[:, s, INV_SUM, t:t + 1]
                                                     ).then_inc(act_f_hi.sem, 1)
                            if gated and t % 2 == 1 and t > 1:
                                exponential(rnd, layer, s, t // 2 - 1)
                            if last_stage and t == T // 2 - 1 and (layer, s) != STEPS[-1]:
                                turned(rnd, *STEPS[step_of(layer, s) + 1])
                                if (layer, s) == (0, 0):
                                    absolute(rnd, 1)

            if ROUNDS > 1:
                with act.Fori(0, ROUNDS - 1) as rnd:
                    one_round(rnd, True)
            one_round(ROUNDS - 1, False)
            act.wait_ge(stored[0], ROUNDS * 16)

        @block.vector
        def _(dve):
            for sig in (dve_bits, dve_masked, dve_row, dve_odd_row, dve_flag, dve_sums, dve_shifted, dve_inv, dve_conv,
                        dve_xt, dve_logit, dve_f, dve_link, dve_last, dve_act, dve_y, dve_stats, dve_mean, dve_x):
                dve.sem_inc(sig.sem, sig.per_round)
            nc.vector.memset(ones[:, :].bitcast(F32), 1.0).then_inc(ones_set, 1)
            dve.wait_ge(load_w, 16 * (MATRICES + 5))
            for j in range(MATRICES):
                dve.wait_ge(w_hi_made, j + 1)
                nc.vector.tensor_tensor(w_lo[:, :, j, :], weight_f32[j // 4][:, j % 4],
                                        w_hi[:, :, j, :].bitcast(F32), ALU.subtract).then_inc(w_lo_made, 1)

            def find_flag(rnd, s):
                for r in range(STAGES):
                    dve.wait_ge(moved[r], moves(rnd, s, T - STAGES + r))
                for m in range(1, T):
                    n = s * (T - 1) + m
                    if m > 1:
                        dve.wait_ge(dve_bits.sem, dve_bits.at(rnd, n - 1))
                    nc.vector.tensor_tensor(seen_bits, seen_bits if m > 1 else adj[s][:, 0, :].bitcast(I32),
                                            adj[s][:, m, :].bitcast(I32), ALU.bitwise_or).then_inc(dve_bits.sem, 1)
                dve.wait_ge(dve_bits.sem, dve_bits.at(rnd, (s + 1) * (T - 1)))
                nc.vector.tensor_scalar(seen_bits, seen_bits, SIGN_OR_LOW_BITS, None,
                                        ALU.bitwise_and).then_inc(dve_masked.sem, 1)
                dve.wait_ge(dve_masked.sem, dve_masked.at(rnd, s + 1))
                nc.vector.tensor_reduce(row_bits[:, :], seen_bits, AX.X, ALU.max,
                                        apply_absolute_value=True).then_inc(dve_row.sem, 1)
                dve.wait_ge(dve_row.sem, dve_row.at(rnd, s + 1))
                dve.wait_ge(pe_flag.sem, pe_flag.at(rnd, s))
                nc.vector.tensor_scalar(odd_row[:, :], row_bits[:, :], 0.0, None,
                                        ALU.not_equal).then_inc(dve_odd_row.sem, 1)
                dve.wait_ge(pe_flag.sem, pe_flag.at(rnd, s + 1))
                nc.vector.tensor_copy(odd_rows[0:1, s:s + 1], count_ps).then_inc(dve_flag.sem, 1)

            def take_sums(rnd, s):
                n = s + 1
                dve.wait_ge(pe_sums.sem, pe_sums.at(rnd, n))
                nc.vector.tensor_copy(sums[:, s], sums_ps).then_inc(dve_sums.sem, 1)
                dve.wait_ge(dve_sums.sem, dve_sums.at(rnd, n))
                nc.vector.tensor_scalar(norms[:, s, INV_SUM, :], sums[:, s, :, 1], ROW_SUM_EPS, None,
                                        ALU.add).then_inc(dve_shifted.sem, 1)
                dve.wait_ge(dve_shifted.sem, dve_shifted.at(rnd, n))
                nc.vector.reciprocal(norms[:, s, INV_SUM, :], norms[:, s, INV_SUM, :]).then_inc(dve_inv.sem, 1)
                dve.wait_ge(dve_inv.sem, dve_inv.at(rnd, n))
                for k in range(1, TAPS):
                    last = nc.vector.tensor_scalar(norms[:, s, CONV + k, :], norms[:, s, INV_SUM, :],
                                                   taps[:, k:k + 1], None, ALU.mult)
                last.then_inc(dve_conv.sem, 1)

            def turned(rnd, layer, s):
                for u in range(PAIRS):
                    dve.wait_ge(act_xt_hi.sem, act_xt_hi.at(rnd, pair_event(layer, s, u)))
                    at = slice(2 * u * P, (2 * u + 2) * P)
                    nc.vector.tensor_tensor(xt_lo[:, :, at], turn_ps[u % 2][:, :, :], xt_hi[:, :, at].bitcast(F32),
                                            ALU.subtract).then_inc(dve_xt.sem, 1)

            def weighted(rnd, layer, s, t):
                source = x_ps[t % 2][:, 0:D]
                dve.wait_ge(pe_x.sem, pe_x.at(rnd, step_of(layer, s) * T + t + 1))
                scale = 1.0
                if layer in GATED:
                    scale = norms[:, s, ABS_NORM if layer == 0 else NORM, t:t + 1]
                    dve.wait_ge(pool_pre.sem, pool_pre.at(rnd, gated_event(layer, s, t // 2) - PAIRS))
                    nc.vector.tensor_tensor(gate[:, t, :], logit_ps,
                                            gate_bias[:, GATED.index(layer), :], ALU.add).then_inc(dve_logit.sem, 1)
                elif layer == CHAIN:
                    before, before_s, _ = step_before(layer, s)
                    if before in GATED:
                        dve.wait_ge(pool_pre.sem, pool_pre.at(rnd, gated_event(before, before_s, t // 2)))
                p = product_of(layer, s)
                dve.wait_ge(act_f_hi.sem, act_f_hi.at(rnd, p * T + t + 1))
                if layer == CHAIN:
                    nc.vector.tensor_scalar(side[:, t, :], source, taps[:, 0:1], taps[:, TAPS:TAPS + 1],
                                            ALU.mult, ALU.add)
                nc.vector.scalar_tensor_tensor(f_lo[:, p % 2, t, :], source, scale,
                                               f_hi[:, p % 2, t, :].bitcast(F32), ALU.mult,
                                               ALU.subtract).then_inc(dve_f.sem, 1)

            def chain_link(rnd, s, stage, t):
                p = product_of(CHAIN, s) + stage
                source = product_bank(CHAIN, s, stage, t)
                last_stage = stage == products_in(CHAIN) - 1
                dve.wait_ge(pe_prod.sem, pe_prod.at(rnd, p * T + t + 1))
                if not last_stage:
                    dve.wait_ge(act_f_hi.sem, act_f_hi.at(rnd, (p + 1) * T + t + 1))
                    nc.vector.scalar_tensor_tensor(f_lo[:, (p + 1) % 2, t, :], source, norms[:, s, INV_SUM, t:t + 1],
                                                   f_hi[:, (p + 1) % 2, t, :].bitcast(F32), ALU.mult,
                                                   ALU.subtract).then_inc(dve_f.sem, 1)
                added = dve_last if last_stage else dve_link
                nc.vector.scalar_tensor_tensor(side[:, t, :], source, norms[:, s, CONV + stage + 1, t:t + 1],
                                               side[:, t, :], ALU.mult, ALU.add).then_inc(added.sem, 1)

            def read_last(rnd, layer, s, t):
                source = product_bank(layer, s, products_in(layer) - 1, t)
                u = t // 2
                if layer == CHAIN:
                    chain_link(rnd, s, products_in(CHAIN) - 1, t)
                    return
                dve.wait_ge(pe_prod.sem, pe_prod.at(rnd, product_of(layer, s) * T + t + 1))
                if layer == LAST:
                    dve.wait_ge(pool_side.sem, pool_side.at(rnd, s * PAIRS + u + 1))
                    if u in (0, PAIRS - 1):
                        done = pair_event(LAST, s, 0)
                        dve.wait_ge(dve_x.sem, dve_x.at(rnd, done if u else done - 1))
                    nc.vector.tensor_tensor(y[:, u % 3, t % 2, :], source, side[:, t, :],
                                            ALU.add).then_inc(dve_last.sem, 1)
                    return
                nc.vector.scalar_tensor_tensor(mixed[:, u % 2, t % 2, :], source,
                                               norms[:, s, ABS_NORM if layer == 0 else NORM, t:t + 1],
                                               side[:, t, :], ALU.mult, ALU.subtract).then_inc(dve_last.sem, 1)

            def residual(rnd, layer, s, u):
                n = step_of(layer, s) * PAIRS + u + 1
                to = y[:, u % 3]
                if layer in GATED:
                    g = gated_event(layer, s, u)
                    dve.wait_ge(pool_pre.sem, pool_pre.at(rnd, g))
                    nc.vector.scalar_tensor_tensor(to, mixed[:, u % 2], 0.0, pair(xs[s], u), ALU.max,
                                                   ALU.add).then_inc(dve_act.sem, 1)
                    dve.wait_ge(dve_act.sem, dve_act.at(rnd, n))
                    dve.wait_ge(act_exp.sem, act_exp.at(rnd, g))
                    nc.vector.scalar_tensor_tensor(to, expo[:, u % 2], -1.0, to, ALU.add,
                                                   ALU.add).then_inc(dve_y.sem, 1)
                elif layer == CHAIN:
                    dve.wait_ge(dve_last.sem, dve_last.at(rnd, last_event(layer, s, 2 * u + 1)))
                    nc.vector.scalar_tensor_tensor(to, pair(side, u), LEAKY_SLOPE, pair(side, u), ALU.mult,
                                                   ALU.max).then_inc(dve_act.sem, 1)
                    dve.wait_ge(dve_act.sem, dve_act.at(rnd, n))
                    nc.vector.tensor_tensor(to, to, pair(xs[s], u), ALU.add).then_inc(dve_y.sem, 1)
                if layer == LAST:
                    dve.wait_ge(dve_last.sem, dve_last.at(rnd, last_event(layer, s, 2 * u + 1)))
                else:
                    dve.wait_ge(dve_y.sem, dve_y.at(rnd, n))
                dve.wait_ge(dve_mean.sem, dve_mean.at(rnd, n - 1))
                for j in range(2):
                    ins = nc.vector.bn_stats(stats[:, j, :], to[:, j, :])
                ins.then_inc(dve_stats.sem, 1)
                wait_apart(dve, dve_stats.sem, dve_stats.at(rnd, n))
                for j in range(2):
                    ins = nc.vector.bn_aggr(mean_var[:, 2 * u + j, :], stats[:, j, :])
                ins.then_inc(dve_mean.sem, 1)

            def normalise(rnd, layer, s, u):
                n = step_of(layer, s) * PAIRS + u + 1
                dve.wait_ge(pool_rstd.sem, pool_rstd.at(rnd, n))
                for j in range(2):
                    t = 2 * u + j
                    ins = nc.vector.tensor_scalar(xs[s][:, t, :], y[:, u % 3, j, :], mean_var[:, t, 0:1],
                                                  rstd[:, t:t + 1], ALU.subtract, ALU.mult)
                ins.then_inc(dve_x.sem, 1)

            with dve.Fori(0, ROUNDS) as rnd:
                turned(rnd, 0, 0)
                find_flag(rnd, 0)
                take_sums(rnd, 0)
                dve.wait_ge(pool_norm.sem, pool_norm.at(rnd, 1))
                for layer, s in STEPS:
                    before = STEPS[step_of(layer, s) - 1] if step_of(layer, s) else None
                    for t in range(T):
                        weighted(rnd, layer, s, t)
                        if before and t == 1:
                            residual(rnd, *before, PAIRS - 1)
                            normalise(rnd, *before, PAIRS - 2)
                        if before and t == 3:
                            normalise(rnd, *before, PAIRS - 1)
                    if layer == CHAIN:
                        for stage in range(products_in(CHAIN) - 1):
                            for t in range(T):
                                chain_link(rnd, s, stage, t)
                    for u in range(PAIRS):
                        for t in (2 * u, 2 * u + 1):
                            read_last(rnd, layer, s, t)
                        if u >= 1:
                            residual(rnd, layer, s, u - 1)
                        if u >= 2:
                            normalise(rnd, layer, s, u - 2)
                        if u == PAIRS // 2 - 1 and (layer, s) != STEPS[-1]:
                            turned(rnd, *STEPS[step_of(layer, s) + 1])
                            if (layer, s) == (0, 0):
                                find_flag(rnd, 1)
                                take_sums(rnd, 1)
                                dve.wait_ge(pool_norm.sem, pool_norm.at(rnd, 2))
                residual(rnd, *STEPS[-1], PAIRS - 1)
                normalise(rnd, *STEPS[-1], PAIRS - 2)
                normalise(rnd, *STEPS[-1], PAIRS - 1)

        @block.gpsimd
        def _(pool):
            for sig in (pool_shifted, pool_norm, pool_gate, pool_mul, pool_pre, pool_side, pool_var, pool_rstd):
                pool.sem_inc(sig.sem, sig.per_round)
            nc.gpsimd.memset(identity[:, :], 0.0).then_inc(identity_steps, 1)
            pool.wait_ge(identity_steps, 1)
            nc.gpsimd.affine_select(out=identity[:, :], in_=identity[:, :], compare_op=ALU.not_equal, fill=1.0,
                                    base=0, pattern=[[-1, P]], channel_multiplier=1).then_inc(identity_steps, 1)
            nc.gpsimd.memset(minus_half[:, :], -0.5).then_inc(half_set, 1)
            pool.wait_ge(half_set, 1)
            pool.wait_ge(load_w, 16 * (MATRICES + 5))

            def find_norms(rnd, s):
                wait_apart(pool, dve_sums.sem, dve_sums.at(rnd, s + 1))
                for j, col in enumerate((ABS_NORM, NORM)):
                    nc.gpsimd.tensor_scalar(norms[:, s, col, :], sums[:, s, :, j], DEGREE_EPS, None,
                                            ALU.add).then_inc(pool_shifted.sem, 1)
                pool.wait_ge(pool_shifted.sem, pool_shifted.at(rnd, 2 * s + 2))
                for col in (ABS_NORM, NORM):
                    last = nc.gpsimd.tensor_tensor(norms[:, s, col, :], norms[:, s, col, :], minus_half[:, :], ALU.pow)
                last.then_inc(pool_norm.sem, 1)

            def gates(rnd, layer, s, u):
                wait_apart(pool, act_gate.sem, act_gate.at(rnd, gated_step_of(layer, s) * T + 2 * u + 2))
                nc.gpsimd.tensor_scalar(pair(gate, u), pair(gate, u), 0.5, 0.5, ALU.mult,
                                        ALU.add).then_inc(pool_gate.sem, 1)

            def mix(rnd, layer, s, u):
                g = gated_event(layer, s, u)
                pool.wait_ge(dve_last.sem, dve_last.at(rnd, last_event(layer, s, 2 * u + 1)))
                pool.wait_ge(pool_gate.sem, pool_gate.at(rnd, g))
                nc.gpsimd.tensor_tensor(mixed[:, u % 2], mixed[:, u % 2], pair(gate, u),
                                        ALU.mult).then_inc(pool_mul.sem, 1)
                pool.wait_ge(pool_mul.sem, pool_mul.at(rnd, g))
                nc.gpsimd.tensor_tensor(mixed[:, u % 2], mixed[:, u % 2], pair(side, u), ALU.add).then_inc(pool_pre.sem, 1)

            def inverse_deviation(rnd, layer, s, u):
                n = pair_event(layer, s, u)
                wait_apart(pool, dve_mean.sem, dve_mean.at(rnd, n))
                at = rstd[:, 2 * u:2 * u + 2]
                nc.gpsimd.tensor_scalar(at, mean_var[:, 2 * u:2 * u + 2, 1], LN_EPS, None, ALU.add).then_inc(pool_var.sem, 1)
                pool.wait_ge(pool_var.sem, pool_var.at(rnd, n))
                nc.gpsimd.tensor_tensor(at, at, minus_half[:, 0:2], ALU.pow).then_inc(pool_rstd.sem, 1)

            def biased(rnd, s, u):
                before, before_s, _ = step_before(LAST, s)
                pool.wait_ge(dve_x.sem, dve_x.at(rnd, pair_event(LAST - 1, s, u)))
                if before == LAST:
                    pool.wait_ge(dve_last.sem, dve_last.at(rnd, last_event(before, before_s, 2 * u + 1)))
                else:
                    pool.wait_ge(pool_pre.sem, pool_pre.at(rnd, gated_event(before, before_s, u)))
                for t in (2 * u, 2 * u + 1):
                    last = nc.gpsimd.tensor_tensor(side[:, t, :], xs[s][:, t, :], last_bias[:, :], ALU.add)
                last.then_inc(pool_side.sem, 1)

            with pool.Fori(0, ROUNDS) as rnd:
                find_norms(rnd, 0)
                for layer, s in STEPS:
                    before = STEPS[step_of(layer, s) - 1] if step_of(layer, s) else None
                    if before and before[0] in GATED:
                        mix(rnd, *before, PAIRS - 1)
                    for u in range(PAIRS):
                        if layer == LAST:
                            biased(rnd, s, u)
                        if layer in GATED:
                            gates(rnd, layer, s, u)
                        if before and u == 0:
                            inverse_deviation(rnd, *before, PAIRS - 1)
                    for u in range(PAIRS):
                        if u == PAIRS // 2 and (layer, s) == (0, 0):
                            find_norms(rnd, 1)
                        if layer in GATED and u < PAIRS - 1:
                            mix(rnd, layer, s, u)
                        if u >= 1:
                            inverse_deviation(rnd, layer, s, u - 1)
                inverse_deviation(rnd, *STEPS[-1], PAIRS - 1)


INPUTS = ["x", "adj", "L0_gnn_theta", "L0_gnn_W_h", "L0_gnn_W_t", "L0_gnn_b_t", "L1_gnn_W", "L1_gnn_conv_w",
          "L1_gnn_conv_b", "L2_gnn_W_t", "L2_gnn_b_t", "L2_gnn_W_h", "L2_gnn_theta", "L3_gnn_weight", "L3_gnn_bias"]
TRANSPOSED = {"adj": (0, 2, 1), "L1_gnn_W": (1, 0)}


def kernel(**inputs):
    import numpy as np
    import concourse.bacc as bacc
    from concourse.bass_utils import run_bass_kernel_spmd

    nc = bacc.Bacc("TRN2", target_bir_lowering=False, num_devices=1)
    arrays, args = {}, []
    for name in INPUTS:
        a = np.asarray(inputs[name])
        a = np.ascontiguousarray(a.transpose(TRANSPOSED[name]) if name in TRANSPOSED else a)
        arrays[f"in_{name}"] = a
        args.append(nc.dram_tensor(f"in_{name}", a.shape, mybir.dt.from_np(a.dtype), kind="ExternalInput").ap())
    shape = arrays["in_x"].shape
    args.append(nc.dram_tensor("out", shape, F32, kind="ExternalOutput").ap())
    gnn_stack(nc, *args)
    result = run_bass_kernel_spmd(nc, [arrays], core_ids=[0])
    return result.results[0]["out"]
```

```python
from contextlib import ExitStack

import concourse.bass as bass
from concourse import mybir

F32 = mybir.dt.float32
F32R = mybir.dt.float32r
I32 = mybir.dt.int32
ALU = mybir.AluOpType
ACT = mybir.ActivationFunctionType
AX = mybir.AxisListType

P = 128
SLOTS = 2
LAYERS = 4
GATED = (0, 2)
CHAIN = 1
LAST = 3
LEAKY_SLOPE = 0.2
LN_EPS = 1e-5
DEGREE_EPS = 1e-6
ROW_SUM_EPS = 1e-9
STAGES = 2
PRODUCT_BANKS = 3
SIGN_OR_LOW_BITS = -(1 << 31) + (1 << 12) - 1

LATER_ROUND = [(3, 1), (1, 0), (0, 1), (2, 0), (1, 1), (3, 0), (2, 1), (0, 0)]
FIRST_ROUND = [(0, 0)] + LATER_ROUND[1:]
LAST_ROUND = LATER_ROUND[:-1] + [(3, 1)]
FIRST_MATRIX = (0, 3, 4, 7)
MATRICES = 8
ABS_NORM, NORM, INV_SUM, CONV = 0, 1, 2, 2


def products_in(layer):
    return 3 if layer == CHAIN else 1


class Step:

    def __init__(self, rounds, rnd, place, shift=0):
        if isinstance(rnd, int):
            rnd, shift = rnd + shift, 0
        self.rounds, self.rnd, self.place, self.shift = rounds, rnd, place, shift
        self.layer, self.slot = self.order[place]
        self.last_stage = products_in(self.layer) - 1

    @property
    def order(self):
        if isinstance(self.rnd, int) and self.rnd == 0:
            return FIRST_ROUND
        if isinstance(self.rnd, int) and self.rnd == self.rounds - 1:
            return LAST_ROUND
        return LATER_ROUND

    @property
    def gated(self):
        return self.layer in GATED

    def before(self):
        if self.place:
            return Step(self.rounds, self.rnd, self.place - 1, self.shift)
        if isinstance(self.rnd, int) and self.rnd == 0:
            return None
        return Step(self.rounds, self.rnd, len(LATER_ROUND) - 1, self.shift - 1)

    def after(self):
        if self.place + 1 < len(self.order):
            return Step(self.rounds, self.rnd, self.place + 1, self.shift)
        return None

    def layer_before(self):
        step = self.before()
        while step.slot != self.slot:
            step = step.before()
        return step

    @property
    def apart(self):
        return self.before() is not None and self.before().slot == self.slot

    def gated_before(self):
        step = self.before()
        while step is not None and not step.gated:
            step = step.before()
        return step


class Signal:

    def __init__(self, sem, counts):
        self.sem, self.counts = sem, counts

    def up_to(self, order, place):
        return sum(self.counts.get(layer, 0) for layer, _ in order[:place])

    def at(self, step, n):
        if isinstance(step.rnd, int) and step.rnd == 0:
            return self.up_to(FIRST_ROUND, step.place) + n
        first, later = self.up_to(FIRST_ROUND, len(FIRST_ROUND)), self.up_to(LATER_ROUND, len(LATER_ROUND))
        return step.rnd * later + ((step.shift - 1) * later + first + self.up_to(LATER_ROUND, step.place) + n)


def gnn_stack(nc, x, adj_t, theta0, wh0, wt0, bt0, w1t, conv_w, conv_b, wt2, bt2, wh2, theta2, w3,
              bias3, out):
    B, N, D = x.shape
    T = N // P
    K = D // P
    PAIRS = T // 2
    ROUNDS = B // SLOTS
    TAPS = conv_w.shape[0]
    assert D == 2 * P and T == 8 and TAPS == 4 and B == ROUNDS * SLOTS and ROUNDS >= 2

    with ExitStack() as ctx:
        def sb(name, shape, dt=F32):
            return ctx.enter_context(nc.sbuf_tensor(name, shape, dt))

        def ps(name, shape):
            return ctx.enter_context(nc.psum_tensor(name, shape, F32))

        def sem(name):
            return ctx.enter_context(nc.semaphore(name))

        def signal(name, counts):
            return Signal(sem(name), counts)

        adj = [sb(f"adj{s}", [P, T, N], F32R) for s in range(SLOTS)]
        stage_adj = sb("stage_adj", [P, STAGES, N])
        xs = [sb(f"x{s}", [P, T, D]) for s in range(SLOTS)]
        xt_hi = sb("xt_hi", [P, K, N], F32R)
        xt_lo = sb("xt_lo", [P, K, N], F32R)
        f_hi = sb("f_hi", [P, 2, T, D], F32R)
        f_lo = sb("f_lo", [P, 2, T, D], F32R)
        side = sb("side", [P, T, D])
        gate = sb("gate", [P, T, D])
        w_hi = sb("w_hi", [P, K, MATRICES, D], F32R)
        w_lo = sb("w_lo", [P, K, MATRICES, D], F32R)
        mixed = sb("mixed", [P, 2, 2, D])
        expo = sb("expo", [P, 2, 2, D])
        y = sb("y", [P, 3, 2, D])
        gate_bias = sb("gate_bias", [P, 2, D])
        last_bias = sb("last_bias", [P, D])
        taps = sb("taps", [P, TAPS + 1])
        abs_adj = sb("abs_adj", [P, N])
        masked = abs_adj[:, :].bitcast(I32)
        identity = sb("identity", [P, P])
        ones = sb("ones", [P, 2], F32R)
        minus_half = sb("minus_half", [P, T])
        norms = sb("norms", [P, SLOTS, 6, T])
        sums = sb("sums", [P, SLOTS, T, 2])
        marks = sb("marks", [P, T])
        most = sb("most", [1, 1])
        odd_graph = sb("odd_graph", [1, SLOTS], I32)
        stats = sb("stats", [P, 2, 6])
        mean_var = sb("mean_var", [P, T, 2])
        rstd = sb("rstd", [P, T])
        shift = sb("shift", [P, T])
        weight_f32 = side[:, :, :].rearrange("p (j k) d -> p j k d", k=K), \
            gate[:, :, :].rearrange("p (j k) d -> p j k d", k=K)

        product_ps = [ps(f"product_ps{b}", [P, 2 * D]) for b in range(PRODUCT_BANKS)]
        turn_ps = [ps(f"turn_ps{b}", [P, K, 2 * P]) for b in range(2)]
        x_ps = [ps(f"x_ps{b}", [P, 2 * D]) for b in range(2)]
        logit_ps = ps("logit_ps", [P, 2 * D])
        sums_ps = turn_ps[1][:, 0, 0:2 * T].rearrange("p (t j) -> p t j", j=2)
        marks_ps = turn_ps[0][0:1, 0, 0:T]

        load_w = sem("load_w")
        load_x = [sem(f"load_x{s}") for s in range(SLOTS)]
        staged = [sem(f"staged{r}") for r in range(STAGES)]
        moved = [sem(f"moved{r}") for r in range(STAGES)]
        stored = [sem(f"stored{s}") for s in range(SLOTS)]
        identity_steps = sem("identity_steps")
        ones_set = sem("ones_set")
        half_set = sem("half_set")
        w_hi_made = sem("w_hi_made")
        w_lo_made = sem("w_lo_made")
        waits_apart = sem("waits_apart")

        def every(n):
            return {layer: n for layer in range(LAYERS)}

        def gated(n):
            return {layer: n for layer in GATED}

        f_counts = {layer: products_in(layer) * T for layer in range(LAYERS)}
        start = {0: 1}
        pe_turned = signal("pe_turned", every(PAIRS))
        pe_x = signal("pe_x", every(T))
        pe_product = signal("pe_product", f_counts)
        pe_marks = signal("pe_marks", start)
        pe_sums = signal("pe_sums", start)
        pe_abs_used = signal("pe_abs_used", {0: T})
        act_xt_hi = signal("act_xt_hi", every(PAIRS))
        act_f_hi = signal("act_f_hi", f_counts)
        act_gate = signal("act_gate", gated(T))
        act_relu = signal("act_relu", gated(PAIRS))
        act_exp = signal("act_exp", gated(PAIRS))
        act_x = signal("act_x", every(PAIRS))
        act_mark = signal("act_mark", {0: T})
        act_abs = signal("act_abs", {0: T})
        dve_masked = signal("dve_masked", {0: T})
        dve_most = signal("dve_most", start)
        dve_flag = signal("dve_flag", start)
        dve_sums = signal("dve_sums", start)
        dve_shifted = signal("dve_shifted", start)
        dve_inv = signal("dve_inv", start)
        dve_xt = signal("dve_xt", every(PAIRS))
        dve_logit = signal("dve_logit", gated(T))
        dve_f = signal("dve_f", f_counts)
        dve_link = signal("dve_link", {CHAIN: 2 * T})
        dve_last = signal("dve_last", every(T))
        dve_act = signal("dve_act", {0: PAIRS, 1: PAIRS, 2: PAIRS})
        dve_y = signal("dve_y", {0: PAIRS, 1: PAIRS, 2: PAIRS})
        dve_stats = signal("dve_stats", every(PAIRS))
        dve_mean = signal("dve_mean", every(PAIRS))
        pool_shifted = signal("pool_shifted", {0: 2})
        pool_norm = signal("pool_norm", {0: 2})
        pool_gate = signal("pool_gate", gated(PAIRS))
        pool_mul = signal("pool_mul", gated(PAIRS))
        pool_mix = signal("pool_mix", gated(PAIRS))
        pool_h = signal("pool_h", {CHAIN: PAIRS})
        pool_side = signal("pool_side", {CHAIN: PAIRS, LAST: PAIRS})
        pool_var = signal("pool_var", every(PAIRS))
        pool_rstd = signal("pool_rstd", every(PAIRS))
        pool_shift = signal("pool_shift", every(PAIRS))

        x_dram = x.rearrange("(i s) (t p) d -> i s p t d", s=SLOTS, p=P)
        out_dram = out.rearrange("(i s) (t p) d -> i s p t d", s=SLOTS, p=P)
        adj_dram = adj_t.rearrange("(i s) (t p) n -> i s p t n", s=SLOTS, p=P)

        def all_rounds(engine, one_round):
            one_round(0)
            if ROUNDS > 2:
                with engine.Fori(1, ROUNDS - 1) as rnd:
                    one_round(rnd)
            one_round(ROUNDS - 1)

        def steps_of(rnd):
            return [Step(ROUNDS, rnd, place) for place in range(len(LATER_ROUND))]

        def graph_round(step):
            if (step.layer, step.slot) == (3, 1) and step.place == 0:
                return step.rnd + (step.shift - 1)
            if (step.layer, step.slot) == (0, 0) and step.place:
                return step.rnd + (step.shift + 1)
            return step.rnd + step.shift

        def next_turned(step):
            if step.after() is not None:
                return None if step.after().apart else step.after()
            if isinstance(step.rnd, int) and step.rnd == ROUNDS - 1:
                return None
            return Step(ROUNDS, step.rnd, 0, step.shift + 1)

        def f_buffer(step, stage):
            return (step.place + stage) % 2

        def product_number(step, stage, t):
            return sum(products_in(layer) * T for layer, _ in LATER_ROUND[:step.place]) + stage * T + t

        def product_bank(step, stage, t):
            return product_ps[product_number(step, stage, t) % PRODUCT_BANKS][:, 0:D]

        def x_banks(step):
            idle = product_number(step, 0, 2) % PRODUCT_BANKS
            return x_ps + ([] if step.gated else [logit_ps]) + [product_ps[idle]]

        def x_bank(step, t):
            return x_banks(step)[t % len(x_banks(step))]

        def logit_bank(step, t):
            return (logit_ps, product_ps[product_number(step, 0, 1) % PRODUCT_BANKS])[t % 2][:, 0:D]

        def y_buffer(step, u):
            return y[:, (u + (step.layer == LAST)) % 3]

        def norm_of(step, t):
            return norms[:, step.slot, ABS_NORM if step.layer == 0 else NORM, t:t + 1]

        def moves(rnd, s, m):
            return (rnd * SLOTS + s) * (T // STAGES * 16) + (m // STAGES + 1) * 16

        def looked_at(step, stage, t):
            if step.after() is None or step.after().layer != 0:
                return None
            if step.layer == CHAIN:
                return t if stage == 1 else None
            if stage < 0:
                return {4: 0, 6: 1}.get(t)
            return t + 2 if t + 2 < T else None

        def marked_at(step, stage, t):
            m = looked_at(step, stage, t)
            if step.after() is not None and step.after().layer == 0 and step.layer == CHAIN and (stage, t) == (2, 0):
                return T - 1
            if step.layer != CHAIN and (stage, t) == (0, T - 2) and looked_at(step, 0, T - 3) is not None:
                return T - 1
            return m - 1 if m else None

        def pair(tile, u):
            return tile[:, 2 * u:2 * u + 2, :]

        block = ctx.enter_context(nc.Block())

        @block.sync
        def _(sp):
            def stream(rnd, s, last_use=None):
                def stage(m):
                    if m >= STAGES or last_use is not None or s > 0:
                        sp.wait_ge(moved[m % STAGES], moves(rnd, s, m) - 16)
                        sp.sem_inc(waits_apart, 1)
                    sp.dma_start(stage_adj[:, m % STAGES, :], adj_dram[rnd, s, :, m, :]).then_inc(staged[m % STAGES], 16)

                for m in range(STAGES):
                    stage(m)
                if last_use is not None:
                    sp.wait_ge(pe_product.sem, last_use)
                    sp.sem_inc(waits_apart, 1)
                for m in range(T):
                    sp.wait_ge(staged[m % STAGES], moves(rnd, s, m))
                    sp.sem_inc(waits_apart, 1)
                    sp.dma_start(adj[s][:, m, :].bitcast(F32), stage_adj[:, m % STAGES, :]).then_inc(moved[m % STAGES], 16)
                    if m + STAGES < T:
                        stage(m + STAGES)

            def one_round(rnd):
                for step in steps_of(rnd):
                    if step.layer == LAST and step.order is not LAST_ROUND or \
                            step.layer == LAST and step.place == 0:
                        at = step.rnd if step.slot else step.rnd + 1
                        stream(at, step.slot, pe_product.at(step, T))

            for j, w in enumerate((theta0, wh0, wt0, w1t, theta2, wh2, wt2, w3)):
                sp.dma_start(weight_f32[j // 4][:, j % 4], w.rearrange("(k p) d -> p k d", p=P)).then_inc(load_w, 16)
            for j, b in enumerate((bt0, bt2)):
                sp.dma_start(gate_bias[:, j, :], b.partition_broadcast(P)).then_inc(load_w, 16)
            sp.dma_start(last_bias[:, :], bias3.partition_broadcast(P)).then_inc(load_w, 16)
            sp.dma_start(taps[:, 0:TAPS], conv_w.partition_broadcast(P)).then_inc(load_w, 16)
            sp.dma_start(taps[:, TAPS:TAPS + 1], conv_b.partition_broadcast(P)).then_inc(load_w, 16)
            stream(0, 0)
            stream(0, 1)
            all_rounds(sp, one_round)

        @block.tensor
        def _(pe):
            odd = [pe.alloc_register(f"odd{s}") for s in range(SLOTS)]

            def turn(step, u):
                s = step.slot
                if step.layer == 0:
                    if u == 0:
                        pe.wait_ge(load_x[s], graph_round(step) * 16 + 16)
                        if zero_before(step):
                            pe.wait_ge(dve_sums.sem, dve_sums.at(zero_before(step), 1))
                else:
                    pe.wait_ge(act_x.sem, act_x.at(step.layer_before(), u + 1))
                if u >= 2:
                    pe.wait_ge(dve_xt.sem, dve_xt.at(step, u - 1))
                elif step.before():
                    pe.wait_ge(dve_xt.sem, dve_xt.at(step.before(), PAIRS + u - 1))
                for t in range(2):
                    for k in range(K):
                        last = nc.tensor.transpose(turn_ps[u % 2][:, k, t * P:(t + 1) * P],
                                                   xs[s][:, 2 * u + t, k * P:(k + 1) * P], identity[:, :])
                last.then_inc(pe_turned.sem, 1)

            def zero_before(step):
                step = step.before()
                while step is not None and step.layer != 0:
                    step = step.before()
                return step

            def add_marks(step):
                pe.wait_ge(act_mark.sem, act_mark.at(step, T))
                pe.wait_ge(dve_xt.sem, dve_xt.at(step, PAIRS))
                nc.tensor.matmul(marks_ps, ones[:, 0:1].bitcast(F32), marks[:, :],
                                 start=True, stop=True).then_inc(pe_marks.sem, 1)

            def sum_rows(step, general):
                s = step.slot
                for m in range(T):
                    if general:
                        pe.wait_ge(act_abs.sem, act_abs.at(step, m + 1))
                    for t in range(T):
                        n = slice(t * P, (t + 1) * P)
                        opened = dict(start=(m == 0 and t == 0), stop=(m == T - 1), skip_group_check=True)
                        closed = dict(start=False, stop=(m == T - 1), skip_group_check=True)
                        if general:
                            one = ones[:, 0:1].bitcast(F32)
                            nc.tensor.matmul(sums_ps[:, t, 0:1], abs_adj[:, n], one, **opened)
                            last = nc.tensor.matmul(sums_ps[:, t, 1:2], adj[s][:, m, n].bitcast(F32), one, **closed)
                        else:
                            last = nc.tensor.matmul(sums_ps[:, t, :], adj[s][:, m, n], ones[:, :], **opened)
                    if general:
                        last.then_inc(pe_abs_used.sem, 1)
                if general:
                    pe.wait_ge(pe_abs_used.sem, pe_abs_used.at(step, T))
                    pe.sem_inc(pe_sums.sem, 1)
                else:
                    last.then_inc(pe_sums.sem, 1)
                    pe.sem_inc(pe_abs_used.sem, T)

            def find_sums(step):
                pe.wait_ge(dve_flag.sem, dve_flag.at(step, 1))
                pe.sem_inc(waits_apart, 1)
                pe.reg_load(odd[step.slot], odd_graph[0:1, step.slot:step.slot + 1])
                with pe.If(odd[step.slot]):
                    sum_rows(step, True)
                with pe.Else():
                    sum_rows(step, False)

            def through_weights(step, t):
                first = FIRST_MATRIX[step.layer]
                width = 2 if step.gated else 1
                banks = len(x_banks(step))
                if t % 2 == 0:
                    pe.wait_ge(dve_xt.sem, dve_xt.at(step, t // 2 + 1))
                if t >= banks:
                    pe.wait_ge(dve_f.sem, dve_f.at(step, t - banks + 1))
                elif t == 0 and step.before():
                    pe.wait_ge(dve_f.sem, dve_f.at(step.before(), T))
                elif t == banks - 1 and step.before():
                    pe.wait_ge(dve_last.sem, dve_last.at(step.before(), T))
                tile = slice(t * P, (t + 1) * P)
                parts = [(x_part, w_part, k) for k in range(K)
                         for x_part, w_part in ((xt_hi, w_hi), (xt_hi, w_lo), (xt_lo, w_hi))]
                for n, (x_part, w_part, k) in enumerate(parts):
                    last = nc.tensor.matmul(x_bank(step, t)[:, 0:width * D], x_part[:, k, tile],
                                            w_part[:, k, first:first + width, :],
                                            start=n == 0, stop=n == len(parts) - 1)
                if step.gated:
                    if t >= 2:
                        pe.wait_ge(dve_logit.sem, dve_logit.at(step, t - 1))
                    elif t == 1 and step.before():
                        pe.wait_ge(dve_last.sem, dve_last.at(step.before(), T - 1))
                    for n, (x_part, w_part, k) in enumerate(parts):
                        last = nc.tensor.matmul(logit_bank(step, t), x_part[:, k, tile], w_part[:, k, first + 2, :],
                                                start=n == 0, stop=n == len(parts) - 1)
                last.then_inc(pe_x.sem, 1)

            def bank_free(step, stage, t):
                n = stage * T + t - PRODUCT_BANKS
                if stage == 0 and t == 1 and step.gated:
                    pe.wait_ge(dve_logit.sem, dve_logit.at(step, T))
                    return
                if stage == 0 and t == 2:
                    return
                if n < 0:
                    step = step.before()
                    if step is None:
                        return
                    n += step.last_stage * T + T
                if n < step.last_stage * T:
                    pe.wait_ge(dve_link.sem, dve_link.at(step, n + 1))
                else:
                    pe.wait_ge(dve_last.sem, dve_last.at(step, n - step.last_stage * T + 1))

            def product(step, stage, general):
                blocks = [(m, t) for m in range(T) for t in (0, 1)]
                blocks += [(m, t) for t in range(2, T) for m in range(T)]
                for m, t in blocks:
                    if m == 0:
                        bank_free(step, stage, t)
                    if t == 0:
                        pe.wait_ge(dve_f.sem, dve_f.at(step, stage * T + m + 1))
                    for part in (f_hi, f_lo):
                        f = part[:, f_buffer(step, stage), m, :]
                        block = adj[step.slot][:, m, t * P:(t + 1) * P]
                        if general:
                            block, f = block.bitcast(F32), f.bitcast(F32)
                        last = nc.tensor.matmul(product_bank(step, stage, t), block, f,
                                                start=(m == 0 and part is f_hi),
                                                stop=(m == T - 1 and part is f_lo))
                    if m == T - 1:
                        last.then_inc(pe_product.sem, 1)
                        if stage == step.last_stage and 3 <= t < 3 + PAIRS and next_turned(step):
                            turn(next_turned(step), t - 3)

            def one_round(rnd):
                for step in steps_of(rnd):
                    if step.apart:
                        for u in range(PAIRS):
                            turn(step, u)
                    if step.layer == 0:
                        add_marks(step)
                    for t in range(T):
                        through_weights(step, t)
                        if step.layer == 0 and t == 0:
                            find_sums(step)
                    for stage in range(step.last_stage + 1):
                        with pe.If(odd[step.slot]):
                            product(step, stage, True)
                        with pe.Else():
                            product(step, stage, False)

            pe.wait_ge(identity_steps, 2)
            pe.wait_ge(ones_set, 1)
            pe.wait_ge(w_lo_made, MATRICES)
            for u in range(PAIRS):
                turn(steps_of(0)[0], u)
            all_rounds(pe, one_round)

        @block.scalar
        def _(act):
            def store(step):
                act.wait_ge(act_x.sem, act_x.at(step, PAIRS))
                act.sem_inc(waits_apart, 1)
                act.dma_start(out_dram[graph_round(step), step.slot], xs[step.slot][:, :, :]).then_inc(stored[step.slot], 16)

            def load_next(step):
                at = graph_round(step)
                if isinstance(at, int) and at + 1 == ROUNDS:
                    return
                act.wait_ge(stored[step.slot], at * 16 + 16)
                act.sem_inc(waits_apart, 1)
                act.dma_start(xs[step.slot][:, :, :], x_dram[at + 1, step.slot]).then_inc(load_x[step.slot], 16)

            def turned(step, u):
                act.wait_ge(pe_turned.sem, pe_turned.at(step, u + 1))
                nc.scalar.activation(xt_hi[:, :, 2 * u * P:(2 * u + 2) * P], turn_ps[u % 2][:, :, :],
                                     ACT.Copy).then_inc(act_xt_hi.sem, 1)

            def mark(step, m):
                act.wait_ge(dve_masked.sem, dve_masked.at(step, m + 1))
                nc.scalar.activation(abs_adj[:, :], masked, ACT.Abs,
                                     accum_out=marks[:, m:m + 1]).then_inc(act_mark.sem, 1)

            def absolute(step):
                act.wait_ge(dve_flag.sem, dve_flag.at(step, 1))
                act.sem_inc(waits_apart, 1)
                odd = act.value_load(odd_graph[0:1, step.slot:step.slot + 1])
                with act.If(odd):
                    for m in range(T):
                        if m:
                            act.wait_ge(pe_abs_used.sem, pe_abs_used.at(step, m))
                        nc.scalar.activation(abs_adj[:, :], adj[step.slot][:, m, :].bitcast(F32),
                                             ACT.Abs).then_inc(act_abs.sem, 1)
                with act.Else():
                    act.sem_inc(act_abs.sem, T)

            def tanh(step, t):
                act.wait_ge(dve_logit.sem, dve_logit.at(step, t + 1))
                nc.scalar.activation(gate[:, t, :], gate[:, t, :], ACT.Tanh, scale=0.5).then_inc(act_gate.sem, 1)

            def exponential(step, u):
                act.wait_ge(pool_mix.sem, pool_mix.at(step, u + 1))
                nc.scalar.activation(expo[:, u % 2], mixed[:, u % 2], ACT.Relu, scale=-1.0).then_inc(act_relu.sem, 1)
                act.wait_ge(act_relu.sem, act_relu.at(step, u + 1))
                nc.scalar.activation(expo[:, u % 2], expo[:, u % 2], ACT.Exp, scale=-1.0).then_inc(act_exp.sem, 1)

            def normalise(step, u):
                for t in (2 * u, 2 * u + 1):
                    act.wait_ge(pool_shift.sem, pool_shift.at(step, u + 1))
                    last = nc.scalar.activation(xs[step.slot][:, t, :], y_buffer(step, u)[:, t % 2, :], ACT.Identity,
                                                scale=rstd[:, t:t + 1], bias=shift[:, t:t + 1])
                last.then_inc(act_x.sem, 1)

            def one_round(rnd):
                for step in steps_of(rnd):
                    before = step.before()
                    if step.apart:
                        exponential(before, PAIRS - 1)
                        for u in range(PAIRS):
                            if u:
                                normalise(before, u)
                            turned(step, u)
                    for t in range(T):
                        act.wait_ge(pe_x.sem, pe_x.at(step, t + 1))
                        if step.gated:
                            if before is not None and t % 2 == 0:
                                if before.gated:
                                    act.wait_ge(pool_mix.sem, pool_mix.at(before, t // 2 + 1))
                                elif before.layer == CHAIN:
                                    act.wait_ge(dve_act.sem, dve_act.at(before, t // 2 + 1))
                                else:
                                    act.wait_ge(dve_last.sem, dve_last.at(before, t + 2))
                            nc.scalar.activation(side[:, t, :], x_bank(step, t)[:, D:2 * D], ACT.Copy)
                        if step.layer == 0 and t == 0:
                            absolute(step)
                            act.wait_ge(pool_norm.sem, pool_norm.at(step, 1))
                        nc.scalar.activation(f_hi[:, f_buffer(step, 0), t, :], x_bank(step, t)[:, 0:D], ACT.Copy,
                                             scale=norm_of(step, t) if step.gated else 1.0).then_inc(act_f_hi.sem, 1)
                        if step.gated and t >= 1:
                            tanh(step, t - 1)
                        if before is not None and not step.apart:
                            if before.gated and t == 1:
                                exponential(before, PAIRS - 1)
                            if step.gated and t in (2, 4, 5):
                                normalise(before, (2, 4, 5).index(t) + 1)
                        if before is not None and before.layer == LAST and before.slot == 0 and t == 5:
                            store(before)
                        if marked_at(step, -1, t) is not None:
                            mark(step.after(), marked_at(step, -1, t))
                    if step.gated:
                        tanh(step, T - 1)
                    if before is not None and before.layer == LAST and before.slot == 0:
                        load_next(before)
                    if before is not None and not step.gated and not step.apart:
                        normalise(before, 1)
                        normalise(before, 2)
                    for stage in range(step.last_stage + 1):
                        for t in range(T):
                            if before is not None and not step.gated and not step.apart and stage == 0 and t == 1:
                                normalise(before, 3)
                            if stage < step.last_stage:
                                act.wait_ge(pe_product.sem, pe_product.at(step, stage * T + t + 1))
                                nc.scalar.activation(f_hi[:, f_buffer(step, stage + 1), t, :], product_bank(step, stage, t),
                                                     ACT.Copy, scale=norms[:, step.slot, INV_SUM, t:t + 1]
                                                     ).then_inc(act_f_hi.sem, 1)
                                if before is not None and before.layer == LAST and before.slot == 1 and stage == 0:
                                    if t == 3:
                                        store(before)
                                    if t == 7:
                                        load_next(before)
                            else:
                                if step.gated and t in (3, 5, 7):
                                    exponential(step, t // 2 - 1)
                                if t == (5 if step.layer == LAST else 7):
                                    normalise(step, 0)
                                if next_turned(step) and 3 <= t < 3 + PAIRS:
                                    turned(next_turned(step), t - 3)
                            if marked_at(step, stage, t) is not None:
                                mark(step.after(), marked_at(step, stage, t))

            for s in range(SLOTS):
                act.dma_start(xs[s][:, :, :], x_dram[0, s]).then_inc(load_x[s], 16)
            act.wait_ge(load_w, 16 * (MATRICES + 5))
            for j in range(MATRICES):
                nc.scalar.activation(w_hi[:, :, j, :], weight_f32[j // 4][:, j % 4], ACT.Copy).then_inc(w_hi_made, 1)
            act.wait_ge(w_lo_made, MATRICES)
            for u in range(PAIRS):
                turned(steps_of(0)[0], u)
            for m in range(T):
                mark(steps_of(0)[0], m)
            all_rounds(act, one_round)
            end = steps_of(ROUNDS - 1)[-1]
            for u in range(1, PAIRS):
                normalise(end, u)
            store(end)
            for s in range(SLOTS):
                act.wait_ge(stored[s], ROUNDS * 16)

        @block.vector
        def _(dve):
            def mask(step, m):
                dve.wait_ge(moved[m % STAGES], moves(graph_round(step), step.slot, m))
                if m:
                    dve.wait_ge(act_mark.sem, act_mark.at(step, m))
                nc.vector.tensor_scalar(masked, adj[step.slot][:, m, :].bitcast(I32), SIGN_OR_LOW_BITS, None,
                                        ALU.bitwise_and).then_inc(dve_masked.sem, 1)

            def find_flag(step):
                dve.wait_ge(pe_marks.sem, pe_marks.at(step, 1))
                nc.vector.tensor_reduce(most[:, :], marks_ps, AX.X, ALU.max).then_inc(dve_most.sem, 1)
                dve.wait_ge(dve_most.sem, dve_most.at(step, 1))
                nc.vector.tensor_scalar(odd_graph[0:1, step.slot:step.slot + 1], most[:, :], 0.0, None,
                                        ALU.not_equal).then_inc(dve_flag.sem, 1)

            def take_sums(step):
                s = step.slot
                dve.wait_ge(pe_sums.sem, pe_sums.at(step, 1))
                nc.vector.tensor_copy(sums[:, s], sums_ps).then_inc(dve_sums.sem, 1)
                dve.wait_ge(dve_sums.sem, dve_sums.at(step, 1))
                nc.vector.tensor_scalar(norms[:, s, INV_SUM, :], sums[:, s, :, 1], ROW_SUM_EPS, None,
                                        ALU.add).then_inc(dve_shifted.sem, 1)

            def invert_sums(step):
                s = step.slot
                dve.wait_ge(dve_shifted.sem, dve_shifted.at(step, 1))
                nc.vector.reciprocal(norms[:, s, INV_SUM, :], norms[:, s, INV_SUM, :]).then_inc(dve_inv.sem, 1)
                dve.wait_ge(dve_inv.sem, dve_inv.at(step, 1))
                for k in range(1, TAPS):
                    nc.vector.tensor_scalar(norms[:, s, CONV + k, :], norms[:, s, INV_SUM, :],
                                            taps[:, k:k + 1], None, ALU.mult)

            def turned(step, u):
                dve.wait_ge(act_xt_hi.sem, act_xt_hi.at(step, u + 1))
                at = slice(2 * u * P, (2 * u + 2) * P)
                nc.vector.tensor_tensor(xt_lo[:, :, at], turn_ps[u % 2][:, :, :], xt_hi[:, :, at].bitcast(F32),
                                        ALU.subtract).then_inc(dve_xt.sem, 1)

            def logits(step, t):
                dve.wait_ge(pe_x.sem, pe_x.at(step, t + 1))
                if t % 2 == 0 and step.gated_before():
                    dve.wait_ge(pool_mix.sem, pool_mix.at(step.gated_before(), t // 2 + 1))
                nc.vector.tensor_tensor(gate[:, t, :], logit_bank(step, t), gate_bias[:, GATED.index(step.layer), :],
                                        ALU.add).then_inc(dve_logit.sem, 1)

            def remainder(step, stage, t, source, scale):
                dve.wait_ge(act_f_hi.sem, act_f_hi.at(step, stage * T + t + 1))
                b = f_buffer(step, stage)
                nc.vector.scalar_tensor_tensor(f_lo[:, b, t, :], source, scale, f_hi[:, b, t, :].bitcast(F32),
                                               ALU.mult, ALU.subtract).then_inc(dve_f.sem, 1)

            def chain_link(step, stage, t):
                s = step.slot
                source = product_bank(step, stage, t)
                dve.wait_ge(pe_product.sem, pe_product.at(step, stage * T + t + 1))
                if stage < step.last_stage:
                    remainder(step, stage + 1, t, source, norms[:, s, INV_SUM, t:t + 1])
                if stage == 0 and t % 2 == 0:
                    dve.wait_ge(pool_side.sem, pool_side.at(step, t // 2 + 1))
                added = dve_link if stage < step.last_stage else dve_last
                nc.vector.scalar_tensor_tensor(side[:, t, :], source, norms[:, s, CONV + stage + 1, t:t + 1],
                                               side[:, t, :], ALU.mult, ALU.add).then_inc(added.sem, 1)

            def read_last(step, t):
                source = product_bank(step, step.last_stage, t)
                u = t // 2
                if step.layer == CHAIN:
                    chain_link(step, step.last_stage, t)
                    return
                dve.wait_ge(pe_product.sem, pe_product.at(step, t + 1))
                if step.layer == LAST:
                    if t % 2 == 0:
                        dve.wait_ge(pool_side.sem, pool_side.at(step, u + 1))
                        if u < PAIRS - 1:
                            dve.wait_ge(act_x.sem, act_x.at(step.before(), u + 2))
                        else:
                            dve.wait_ge(act_x.sem, act_x.at(step, 1))
                    nc.vector.tensor_tensor(y_buffer(step, u)[:, t % 2, :], source, side[:, t, :],
                                            ALU.add).then_inc(dve_last.sem, 1)
                    return
                nc.vector.scalar_tensor_tensor(mixed[:, u % 2, t % 2, :], source, norm_of(step, t),
                                               side[:, t, :], ALU.mult, ALU.subtract).then_inc(dve_last.sem, 1)

            def residual(step, u):
                to = y_buffer(step, u)
                x_pair = pair(xs[step.slot], u)
                if step.layer != LAST:
                    if u == 0 and step.before():
                        dve.wait_ge(act_x.sem, act_x.at(step.before(), PAIRS))
                    elif u == PAIRS - 1:
                        dve.wait_ge(act_x.sem, act_x.at(step, 1))
                if step.gated:
                    dve.wait_ge(pool_mix.sem, pool_mix.at(step, u + 1))
                    nc.vector.scalar_tensor_tensor(to, mixed[:, u % 2], 0.0, x_pair, ALU.max,
                                                   ALU.add).then_inc(dve_act.sem, 1)
                    dve.wait_ge(dve_act.sem, dve_act.at(step, u + 1))
                    dve.wait_ge(act_exp.sem, act_exp.at(step, u + 1))
                    nc.vector.scalar_tensor_tensor(to, expo[:, u % 2], -1.0, to, ALU.add,
                                                   ALU.add).then_inc(dve_y.sem, 1)
                elif step.layer == CHAIN:
                    dve.wait_ge(dve_last.sem, dve_last.at(step, 2 * u + 2))
                    nc.vector.scalar_tensor_tensor(to, pair(side, u), LEAKY_SLOPE, pair(side, u), ALU.mult,
                                                   ALU.max).then_inc(dve_act.sem, 1)
                    dve.wait_ge(dve_act.sem, dve_act.at(step, u + 1))
                    nc.vector.tensor_tensor(to, to, x_pair, ALU.add).then_inc(dve_y.sem, 1)
                if step.layer == LAST:
                    dve.wait_ge(dve_last.sem, dve_last.at(step, 2 * u + 2))
                else:
                    dve.wait_ge(dve_y.sem, dve_y.at(step, u + 1))
                if u:
                    dve.wait_ge(dve_mean.sem, dve_mean.at(step, u))
                elif step.before():
                    dve.wait_ge(dve_mean.sem, dve_mean.at(step.before(), PAIRS))
                for j in range(2):
                    last = nc.vector.bn_stats(stats[:, j, :], to[:, j, :])
                last.then_inc(dve_stats.sem, 1)
                dve.wait_ge(dve_stats.sem, dve_stats.at(step, u + 1))
                dve.sem_inc(waits_apart, 1)
                for j in range(2):
                    last = nc.vector.bn_aggr(mean_var[:, 2 * u + j, :], stats[:, j, :])
                last.then_inc(dve_mean.sem, 1)

            def one_round(rnd):
                for step in steps_of(rnd):
                    before = step.before()
                    if step.layer == 0:
                        find_flag(step)
                    if step.apart:
                        residual(before, 2)
                        residual(before, 3)
                        for u in range(PAIRS):
                            turned(step, u)
                    for t in range(T):
                        if step.gated:
                            logits(step, t)
                        else:
                            dve.wait_ge(pe_x.sem, pe_x.at(step, t + 1))
                        if step.layer == 0 and t == 0:
                            take_sums(step)
                        remainder(step, 0, t, x_bank(step, t)[:, 0:D], norm_of(step, t) if step.gated else 1.0)
                        if step.layer == 0 and t == 0:
                            invert_sums(step)
                        if before is not None and not step.apart and t in ((1, 3) if step.gated else (3, 7)):
                            residual(before, 2 + t // (2 if step.gated else 4))
                        if looked_at(step, -1, t) is not None:
                            mask(step.after(), looked_at(step, -1, t))
                    for stage in range(step.last_stage + 1):
                        for t in range(T):
                            if stage < step.last_stage:
                                chain_link(step, stage, t)
                            else:
                                read_last(step, t)
                            if stage == step.last_stage:
                                if t in (3, 5):
                                    residual(step, t // 2 - 1)
                                if next_turned(step) and 3 <= t < 3 + PAIRS:
                                    turned(next_turned(step), t - 3)
                            if looked_at(step, stage, t) is not None:
                                mask(step.after(), looked_at(step, stage, t))

            nc.vector.memset(ones[:, :].bitcast(F32), 1.0).then_inc(ones_set, 1)
            dve.wait_ge(load_w, 16 * (MATRICES + 5))
            for j in range(MATRICES):
                dve.wait_ge(w_hi_made, j + 1)
                nc.vector.tensor_tensor(w_lo[:, :, j, :], weight_f32[j // 4][:, j % 4],
                                        w_hi[:, :, j, :].bitcast(F32), ALU.subtract).then_inc(w_lo_made, 1)
            for u in range(PAIRS):
                turned(steps_of(0)[0], u)
            for m in range(T):
                mask(steps_of(0)[0], m)
            all_rounds(dve, one_round)
            end = steps_of(ROUNDS - 1)[-1]
            residual(end, 2)
            residual(end, 3)

        @block.gpsimd
        def _(pool):
            def find_norms(step):
                s = step.slot
                pool.wait_ge(dve_sums.sem, dve_sums.at(step, 1))
                pool.sem_inc(waits_apart, 1)
                for j, row in enumerate((ABS_NORM, NORM)):
                    nc.gpsimd.tensor_scalar(norms[:, s, row, :], sums[:, s, :, j], DEGREE_EPS, None,
                                            ALU.add).then_inc(pool_shifted.sem, 1)
                for j, row in enumerate((ABS_NORM, NORM)):
                    pool.wait_ge(pool_shifted.sem, pool_shifted.at(step, j + 1))
                    nc.gpsimd.tensor_tensor(norms[:, s, row, :], norms[:, s, row, :], minus_half[:, :],
                                            ALU.pow).then_inc(pool_norm.sem, 1)

            def gates(step, u):
                pool.wait_ge(act_gate.sem, act_gate.at(step, 2 * u + 2))
                pool.sem_inc(waits_apart, 1)
                nc.gpsimd.tensor_scalar(pair(gate, u), pair(gate, u), 0.5, 0.5, ALU.mult,
                                        ALU.add).then_inc(pool_gate.sem, 1)

            def mix(step, u):
                pool.wait_ge(dve_last.sem, dve_last.at(step, 2 * u + 2))
                pool.wait_ge(pool_gate.sem, pool_gate.at(step, u + 1))
                nc.gpsimd.tensor_tensor(mixed[:, u % 2], mixed[:, u % 2], pair(gate, u),
                                        ALU.mult).then_inc(pool_mul.sem, 1)
                pool.wait_ge(pool_mul.sem, pool_mul.at(step, u + 1))
                nc.gpsimd.tensor_tensor(mixed[:, u % 2], mixed[:, u % 2], pair(side, u), ALU.add).then_inc(pool_mix.sem, 1)

            def inverse_deviation(step, u):
                pool.wait_ge(dve_mean.sem, dve_mean.at(step, u + 1))
                pool.sem_inc(waits_apart, 1)
                at = rstd[:, 2 * u:2 * u + 2]
                nc.gpsimd.tensor_scalar(at, mean_var[:, 2 * u:2 * u + 2, 1], LN_EPS, None, ALU.add)
                nc.gpsimd.tensor_scalar(shift[:, 2 * u:2 * u + 2], mean_var[:, 2 * u:2 * u + 2, 0], -1.0, None,
                                        ALU.mult).then_inc(pool_var.sem, 1)
                pool.wait_ge(pool_var.sem, pool_var.at(step, u + 1))
                nc.gpsimd.tensor_tensor(at, at, minus_half[:, 0:2], ALU.pow).then_inc(pool_rstd.sem, 1)
                pool.wait_ge(pool_rstd.sem, pool_rstd.at(step, u + 1))
                nc.gpsimd.tensor_tensor(shift[:, 2 * u:2 * u + 2], shift[:, 2 * u:2 * u + 2], at,
                                        ALU.mult).then_inc(pool_shift.sem, 1)

            def side_free(step, u):
                before = step.before()
                if before.gated:
                    pool.wait_ge(pool_mix.sem, pool_mix.at(before, u + 1))
                elif before.layer == CHAIN:
                    pool.wait_ge(dve_act.sem, dve_act.at(before, u + 1))
                else:
                    pool.wait_ge(dve_last.sem, dve_last.at(before, 2 * u + 2))

            def first_term(step, u):
                pool.wait_ge(dve_f.sem, dve_f.at(step, 2 * u + 2))
                side_free(step, u)
                b = f_buffer(step, 0)
                nc.gpsimd.tensor_tensor(pair(side, u), pair(f_hi[:, b].bitcast(F32), u), pair(f_lo[:, b].bitcast(F32), u),
                                        ALU.add).then_inc(pool_h.sem, 1)
                pool.wait_ge(pool_h.sem, pool_h.at(step, u + 1))
                pool.sem_inc(waits_apart, 1)
                nc.gpsimd.tensor_scalar(pair(side, u), pair(side, u), taps[:, 0:1], taps[:, TAPS:TAPS + 1], ALU.mult,
                                        ALU.add).then_inc(pool_side.sem, 1)

            def biased(step, u):
                pool.wait_ge(act_x.sem, act_x.at(step.layer_before(), u + 1))
                side_free(step, u)
                for t in (2 * u, 2 * u + 1):
                    last = nc.gpsimd.tensor_tensor(side[:, t, :], xs[step.slot][:, t, :], last_bias[:, :], ALU.add)
                last.then_inc(pool_side.sem, 1)

            def one_round(rnd):
                for step in steps_of(rnd):
                    before = step.before()
                    if step.layer == 0:
                        find_norms(step)
                    if before is not None and before.gated:
                        mix(before, PAIRS - 1)
                    if before is not None and (step.gated or step.apart):
                        inverse_deviation(before, 2)
                    if step.apart:
                        inverse_deviation(before, 3)
                    for u in range(PAIRS):
                        if step.layer == LAST:
                            biased(step, u)
                        if step.layer == CHAIN:
                            first_term(step, u)
                        if step.gated:
                            gates(step, u)
                        elif not step.apart and u in (1, 3):
                            inverse_deviation(before, 2 + u // 2)
                        if before is not None and step.gated and u == 0:
                            inverse_deviation(before, 3)
                    if step.gated:
                        mix(step, 0)
                        mix(step, 1)
                    inverse_deviation(step, 0)
                    if step.gated:
                        mix(step, 2)
                    inverse_deviation(step, 1)

            nc.gpsimd.memset(identity[:, :], 0.0).then_inc(identity_steps, 1)
            pool.wait_ge(identity_steps, 1)
            nc.gpsimd.affine_select(out=identity[:, :], in_=identity[:, :], compare_op=ALU.not_equal, fill=1.0,
                                    base=0, pattern=[[-1, P]], channel_multiplier=1).then_inc(identity_steps, 1)
            nc.gpsimd.memset(minus_half[:, :], -0.5).then_inc(half_set, 1)
            pool.wait_ge(half_set, 1)
            pool.wait_ge(load_w, 16 * (MATRICES + 5))
            all_rounds(pool, one_round)
            end = steps_of(ROUNDS - 1)[-1]
            inverse_deviation(end, 2)
            inverse_deviation(end, 3)


INPUTS = ["x", "adj", "L0_gnn_theta", "L0_gnn_W_h", "L0_gnn_W_t", "L0_gnn_b_t", "L1_gnn_W", "L1_gnn_conv_w",
          "L1_gnn_conv_b", "L2_gnn_W_t", "L2_gnn_b_t", "L2_gnn_W_h", "L2_gnn_theta", "L3_gnn_weight", "L3_gnn_bias"]
TRANSPOSED = {"adj": (0, 2, 1), "L1_gnn_W": (1, 0)}


def kernel(**inputs):
    import numpy as np
    import concourse.bacc as bacc
    from concourse.bass_utils import run_bass_kernel_spmd

    nc = bacc.Bacc("TRN2", target_bir_lowering=False, num_devices=1)
    arrays, args = {}, []
    for name in INPUTS:
        a = np.asarray(inputs[name])
        a = np.ascontiguousarray(a.transpose(TRANSPOSED[name]) if name in TRANSPOSED else a)
        arrays[f"in_{name}"] = a
        args.append(nc.dram_tensor(f"in_{name}", a.shape, mybir.dt.from_np(a.dtype), kind="ExternalInput").ap())
    shape = arrays["in_x"].shape
    args.append(nc.dram_tensor("out", shape, F32, kind="ExternalOutput").ap())
    gnn_stack(nc, *args)
    result = run_bass_kernel_spmd(nc, [arrays], core_ids=[0])
    return result.results[0]["out"]
```

```python
from contextlib import ExitStack

import concourse.bass as bass
from concourse import mybir

F32 = mybir.dt.float32
F32R = mybir.dt.float32r
I32 = mybir.dt.int32
ALU = mybir.AluOpType
ACT = mybir.ActivationFunctionType
AX = mybir.AxisListType

P = 128
SLOTS = 2
LAYERS = 4
GATED = (0, 2)
CHAIN = 1
LAST = 3
LEAKY_SLOPE = 0.2
LN_EPS = 1e-5
DEGREE_EPS = 1e-6
ROW_SUM_EPS = 1e-9
STAGES = 4
PRODUCT_BANKS = 3
SIGN_OR_LOW_BITS = -(1 << 31) + (1 << 12) - 1

LATER_ROUND = [(3, 1), (1, 0), (0, 1), (2, 0), (1, 1), (3, 0), (2, 1), (0, 0)]
FIRST_ROUND = [(0, 0)] + LATER_ROUND[1:]
LAST_ROUND = LATER_ROUND[:-1] + [(3, 1)]
FIRST_MATRIX = (0, 3, 4, 7)
MATRICES = 8
ABS_NORM, NORM, INV_SUM, CONV = 0, 1, 2, 2


def products_in(layer):
    return 3 if layer == CHAIN else 1


class Step:

    def __init__(self, rounds, rnd, place, shift=0):
        if isinstance(rnd, int):
            rnd, shift = rnd + shift, 0
        self.rounds, self.rnd, self.place, self.shift = rounds, rnd, place, shift
        self.layer, self.slot = self.order[place]
        self.last_stage = products_in(self.layer) - 1

    @property
    def order(self):
        if isinstance(self.rnd, int) and self.rnd == 0:
            return FIRST_ROUND
        if isinstance(self.rnd, int) and self.rnd == self.rounds - 1:
            return LAST_ROUND
        return LATER_ROUND

    @property
    def gated(self):
        return self.layer in GATED

    def before(self):
        if self.place:
            return Step(self.rounds, self.rnd, self.place - 1, self.shift)
        if isinstance(self.rnd, int) and self.rnd == 0:
            return None
        return Step(self.rounds, self.rnd, len(LATER_ROUND) - 1, self.shift - 1)

    def after(self):
        if self.place + 1 < len(self.order):
            return Step(self.rounds, self.rnd, self.place + 1, self.shift)
        return None

    def layer_before(self):
        step = self.before()
        while step.slot != self.slot:
            step = step.before()
        return step

    @property
    def apart(self):
        return self.before() is not None and self.before().slot == self.slot

    def gated_before(self):
        step = self.before()
        while step is not None and not step.gated:
            step = step.before()
        return step


class Signal:

    def __init__(self, sem, counts):
        self.sem, self.counts = sem, counts

    def up_to(self, order, place):
        return sum(self.counts.get(layer, 0) for layer, _ in order[:place])

    def at(self, step, n):
        if isinstance(step.rnd, int) and step.rnd == 0:
            return self.up_to(FIRST_ROUND, step.place) + n
        first, later = self.up_to(FIRST_ROUND, len(FIRST_ROUND)), self.up_to(LATER_ROUND, len(LATER_ROUND))
        return step.rnd * later + ((step.shift - 1) * later + first + self.up_to(LATER_ROUND, step.place) + n)


def gnn_stack(nc, x, adj_t, theta0, wh0, wt0, bt0, w1t, conv_w, conv_b, wt2, bt2, wh2, theta2, w3,
              bias3, out):
    B, N, D = x.shape
    T = N // P
    K = D // P
    PAIRS = T // 2
    ROUNDS = B // SLOTS
    TAPS = conv_w.shape[0]
    HALF = N // 2
    HALVES = 2 * T
    assert D == 2 * P and T == 8 and TAPS == 4 and B == ROUNDS * SLOTS and ROUNDS >= 2

    with ExitStack() as ctx:
        def sb(name, shape, dt=F32):
            return ctx.enter_context(nc.sbuf_tensor(name, shape, dt))

        def ps(name, shape):
            return ctx.enter_context(nc.psum_tensor(name, shape, F32))

        def sem(name):
            return ctx.enter_context(nc.semaphore(name))

        def signal(name, counts):
            return Signal(sem(name), counts)

        adj = [sb(f"adj{s}", [P, T, N], F32R) for s in range(SLOTS)]
        stage_adj = sb("stage_adj", [P, STAGES, HALF])
        xs = [sb(f"x{s}", [P, T, D]) for s in range(SLOTS)]
        xt_hi = sb("xt_hi", [P, K, N], F32R)
        xt_lo = sb("xt_lo", [P, K, N], F32R)
        f_hi = sb("f_hi", [P, 2, T, D], F32R)
        f_lo = sb("f_lo", [P, 2, T, D], F32R)
        side = sb("side", [P, T, D])
        gate = sb("gate", [P, T, D])
        w_hi = sb("w_hi", [P, K, MATRICES, D], F32R)
        w_lo = sb("w_lo", [P, K, MATRICES, D], F32R)
        mixed = sb("mixed", [P, 2, 2, D])
        expo = sb("expo", [P, 2, 2, D])
        y = sb("y", [P, 3, 2, D])
        gate_bias = sb("gate_bias", [P, 2, D])
        last_bias = sb("last_bias", [P, D])
        taps = sb("taps", [P, TAPS + 1])
        abs_adj = sb("abs_adj", [P, N])
        masked = abs_adj[:, :].bitcast(I32)
        sums_row = abs_adj[0:1, :]
        identity = sb("identity", [P, P])
        ones = sb("ones", [P, 2], F32R)
        minus_half = sb("minus_half", [P, T])
        norms = sb("norms", [P, SLOTS, 6, T])
        sums = sb("sums", [P, SLOTS, T, 2])
        marks = sb("marks", [P, T])
        most = sb("most", [1, 1])
        odd_graph = sb("odd_graph", [1, SLOTS], I32)
        stats = sb("stats", [P, 2, 6])
        mean_var = sb("mean_var", [P, T, 2])
        rstd = sb("rstd", [P, T])
        shift = sb("shift", [P, T])
        weight_f32 = side[:, :, :].rearrange("p (j k) d -> p j k d", k=K), \
            gate[:, :, :].rearrange("p (j k) d -> p j k d", k=K)

        product_ps = [ps(f"product_ps{b}", [P, 2 * D]) for b in range(PRODUCT_BANKS)]
        turn_ps = [ps(f"turn_ps{b}", [P, K, 2 * P]) for b in range(2)]
        x_ps = [ps(f"x_ps{b}", [P, 2 * D]) for b in range(2)]
        logit_ps = ps("logit_ps", [P, 2 * D])
        rows_ps = [turn_ps[h][0:2, :, :].rearrange("p k n -> p (k n)") for h in range(2)]
        sums_ps = turn_ps[1][:, 0, 0:2 * T].rearrange("p (t j) -> p t j", j=2)
        marks_ps = logit_ps[0:1, D:D + T]

        load_w = sem("load_w")
        load_x = [sem(f"load_x{s}") for s in range(SLOTS)]
        staged = [sem(f"staged{r}") for r in range(STAGES)]
        moved = [sem(f"moved{r}") for r in range(STAGES)]
        stored = [sem(f"stored{s}") for s in range(SLOTS)]
        identity_steps = sem("identity_steps")
        ones_set = sem("ones_set")
        half_set = sem("half_set")
        w_hi_made = sem("w_hi_made")
        w_lo_made = sem("w_lo_made")
        waits_apart = sem("waits_apart")

        def every(n):
            return {layer: n for layer in range(LAYERS)}

        def gated(n):
            return {layer: n for layer in GATED}

        f_counts = {layer: products_in(layer) * T for layer in range(LAYERS)}
        start = {0: 1}
        pe_turned = signal("pe_turned", every(PAIRS))
        pe_x = signal("pe_x", every(T))
        pe_logit = signal("pe_logit", gated(T))
        pe_product = signal("pe_product", f_counts)
        pe_marks = signal("pe_marks", start)
        pe_rows = signal("pe_rows", {0: 2})
        pe_sums = signal("pe_sums", start)
        pe_abs_used = signal("pe_abs_used", {0: T})
        act_xt_hi = signal("act_xt_hi", every(PAIRS))
        act_f_hi = signal("act_f_hi", f_counts)
        act_gate = signal("act_gate", gated(T))
        act_relu = signal("act_relu", gated(PAIRS))
        act_exp = signal("act_exp", gated(PAIRS))
        act_x = signal("act_x", every(PAIRS))
        act_mark = signal("act_mark", {0: T})
        act_abs = signal("act_abs", {0: T})
        act_rows = signal("act_rows", {0: 2})
        dve_masked = signal("dve_masked", {0: T})
        dve_most = signal("dve_most", start)
        dve_flag = signal("dve_flag", start)
        dve_sums = signal("dve_sums", start)
        dve_shifted = signal("dve_shifted", start)
        dve_inv = signal("dve_inv", start)
        dve_xt = signal("dve_xt", every(PAIRS))
        dve_logit = signal("dve_logit", gated(T))
        dve_f = signal("dve_f", f_counts)
        dve_link = signal("dve_link", {CHAIN: 2 * T})
        dve_last = signal("dve_last", every(T))
        dve_act = signal("dve_act", {0: PAIRS, 1: PAIRS, 2: PAIRS})
        dve_y = signal("dve_y", {0: PAIRS, 1: PAIRS, 2: PAIRS})
        dve_stats = signal("dve_stats", every(PAIRS))
        dve_mean = signal("dve_mean", every(PAIRS))
        pool_shifted = signal("pool_shifted", {0: 3})
        pool_norm = signal("pool_norm", {0: 3})
        pool_gate = signal("pool_gate", gated(PAIRS))
        pool_mul = signal("pool_mul", gated(PAIRS))
        pool_mix = signal("pool_mix", gated(PAIRS))
        pool_h = signal("pool_h", {CHAIN: PAIRS})
        pool_side = signal("pool_side", {CHAIN: PAIRS, LAST: PAIRS})
        pool_var = signal("pool_var", every(PAIRS))
        pool_rstd = signal("pool_rstd", every(PAIRS))
        pool_shift = signal("pool_shift", every(PAIRS))

        x_dram = x.rearrange("(i s) (t p) d -> i s p t d", s=SLOTS, p=P)
        out_dram = out.rearrange("(i s) (t p) d -> i s p t d", s=SLOTS, p=P)
        adj_dram = adj_t.rearrange("(i s) (t p) n -> i s p t n", s=SLOTS, p=P)

        def all_rounds(engine, one_round):
            one_round(0)
            if ROUNDS > 2:
                with engine.Fori(1, ROUNDS - 1) as rnd:
                    one_round(rnd)
            one_round(ROUNDS - 1)

        def steps_of(rnd):
            return [Step(ROUNDS, rnd, place) for place in range(len(LATER_ROUND))]

        def graph_round(step):
            if (step.layer, step.slot) == (3, 1) and step.place == 0:
                return step.rnd + (step.shift - 1)
            if (step.layer, step.slot) == (0, 0) and step.place:
                return step.rnd + (step.shift + 1)
            return step.rnd + step.shift

        def next_turned(step):
            if step.after() is not None:
                return None if step.after().apart else step.after()
            if isinstance(step.rnd, int) and step.rnd == ROUNDS - 1:
                return None
            return Step(ROUNDS, step.rnd, 0, step.shift + 1)

        def f_buffer(step, stage):
            return (step.place + stage) % 2

        def product_number(step, stage, t):
            return sum(products_in(layer) * T for layer, _ in LATER_ROUND[:step.place]) + stage * T + t

        def product_bank(step, stage, t):
            return product_ps[product_number(step, stage, t) % PRODUCT_BANKS][:, 0:D]

        def idle_bank(step, t):
            return product_ps[product_number(step, 0, t) % PRODUCT_BANKS]

        def x_banks(step):
            return x_ps + ([idle_bank(step, 1)] if step.gated else [logit_ps, idle_bank(step, 2)])

        def x_bank(step, t):
            return x_banks(step)[t % len(x_banks(step))]

        def logit_bank(step, t):
            return (logit_ps, idle_bank(step, 2))[t % 2][:, 0:D]

        def y_buffer(step, u):
            return y[:, (u + (step.layer == LAST)) % 3]

        def norm_of(step, t):
            return norms[:, step.slot, ABS_NORM if step.layer == 0 else NORM, t:t + 1]

        def moves(rnd, s, h):
            return (rnd * SLOTS + s) * (HALVES // STAGES * 16) + (h // STAGES + 1) * 16

        def columns(h):
            return slice(h // T * HALF, h // T * HALF + HALF)

        LOOKS = {2: {(-1, 0): 0, (-1, 2): 1, (-1, 4): 2, (-1, 5): 3, (-1, 7): 4, (0, 0): 5, (0, 1): 6, (0, 2): 7},
                 CHAIN: {(0, 4): 0, (0, 5): 1, (0, 6): 2, (0, 7): 3, (1, 1): 4, (1, 3): 5, (1, 5): 6, (1, 7): 7}}
        MARKS = {2: {(-1, 1): 0, (-1, 3): 1, (-1, 5): 2, (-1, 6): 3, (0, 0): 4, (0, 1): 5, (0, 2): 6, (0, 3): 7},
                 CHAIN: {(0, 5): 0, (0, 6): 1, (0, 7): 2, (1, 0): 3, (1, 2): 4, (1, 4): 5, (1, 6): 6, (2, 0): 7}}
        FLAG_TILE = 6

        def residual_places(step):
            if not step.gated:
                return 3, 7
            return (0, 1) if step.before().layer == LAST else (1, 3)

        def normalise_places(step):
            return (1, 2, 3) if step.before().layer == LAST else (2, 4, 5)

        def looked_at(step, stage, t):
            return LOOKS[step.layer].get((stage, t)) if step.after() and step.after().layer == 0 else None

        def marked_at(step, stage, t):
            return MARKS[step.layer].get((stage, t)) if step.after() and step.after().layer == 0 else None

        def pair(tile, u):
            return tile[:, 2 * u:2 * u + 2, :]

        block = ctx.enter_context(nc.Block())

        @block.sync
        def _(sp):
            def stream(rnd, s, last=None):

                def stage(h):
                    if h >= STAGES or last is not None or s > 0:
                        sp.wait_ge(moved[h % STAGES], moves(rnd, s, h) - 16)
                        sp.sem_inc(waits_apart, 1)
                    sp.dma_start(stage_adj[:, h % STAGES, :],
                                 adj_dram[rnd, s, :, h % T, columns(h)]).then_inc(staged[h % STAGES], 16)

                for h in range(STAGES):
                    stage(h)
                for h in range(HALVES):
                    if last is not None and h % T == 0:
                        sp.wait_ge(pe_product.sem, pe_product.at(last, (h // T + 1) * T // 2))
                        sp.sem_inc(waits_apart, 1)
                    sp.wait_ge(staged[h % STAGES], moves(rnd, s, h))
                    sp.sem_inc(waits_apart, 1)
                    sp.dma_start(adj[s][:, h % T, columns(h)].bitcast(F32),
                                 stage_adj[:, h % STAGES, :]).then_inc(moved[h % STAGES], 16)
                    if 1 <= h and h - 1 + STAGES < HALVES:
                        stage(h - 1 + STAGES)

            def one_round(rnd):
                for step in steps_of(rnd):
                    if step.layer == LAST and step.order is not LAST_ROUND or \
                            step.layer == LAST and step.place == 0:
                        at = step.rnd if step.slot else step.rnd + 1
                        stream(at, step.slot, step)

            stream(0, 0)
            stream(0, 1)
            all_rounds(sp, one_round)

        @block.tensor
        def _(pe):
            X_AHEAD = 2
            odd = [pe.alloc_register(f"odd{s}") for s in range(SLOTS)]

            def turn(step, u):
                s = step.slot
                if step.layer == 0:
                    if u == 0:
                        pe.wait_ge(load_x[s], graph_round(step) * 16 + 16)
                else:
                    pe.wait_ge(act_x.sem, act_x.at(step.layer_before(), u + 1))
                if u >= 2:
                    pe.wait_ge(dve_xt.sem, dve_xt.at(step, u - 1))
                elif step.before():
                    pe.wait_ge(dve_xt.sem, dve_xt.at(step.before(), PAIRS + u - 1))
                for t in range(2):
                    for k in range(K):
                        last = nc.tensor.transpose(turn_ps[u % 2][:, k, t * P:(t + 1) * P],
                                                   xs[s][:, 2 * u + t, k * P:(k + 1) * P], identity[:, :])
                last.then_inc(pe_turned.sem, 1)

            def add_marks(step):
                pe.wait_ge(act_mark.sem, act_mark.at(step, T))
                nc.tensor.matmul(marks_ps, ones[:, 0:1].bitcast(F32), marks[:, :],
                                 start=True, stop=True).then_inc(pe_marks.sem, 1)

            def sum_odd(step):
                one = ones[:, 0:1].bitcast(F32)
                pe.wait_ge(dve_xt.sem, dve_xt.at(step, PAIRS))
                for m in range(T):
                    pe.wait_ge(act_abs.sem, act_abs.at(step, m + 1))
                    for t in range(T):
                        n = slice(t * P, (t + 1) * P)
                        nc.tensor.matmul(sums_ps[:, t, 0:1], abs_adj[:, n], one, start=(m == 0 and t == 0),
                                         stop=(m == T - 1), skip_group_check=True)
                        last = nc.tensor.matmul(sums_ps[:, t, 1:2], adj[step.slot][:, m, n].bitcast(F32), one,
                                                start=False, stop=(m == T - 1), skip_group_check=True)
                    last.then_inc(pe_abs_used.sem, 1)
                pe.sem_inc(pe_rows.sem, 2)

            def sum_plain(step):
                for h in range(2):
                    pe.wait_ge(dve_xt.sem, dve_xt.at(step, PAIRS - 1 + h))
                    for m in range(T):
                        last = nc.tensor.matmul(rows_ps[h], ones[:, :], adj[step.slot][:, m, h * HALF:(h + 1) * HALF],
                                                start=(m == 0), stop=(m == T - 1))
                    last.then_inc(pe_rows.sem, 1)
                pe.sem_inc(pe_abs_used.sem, T)

            def start_sums(step):
                pe.wait_ge(dve_flag.sem, dve_flag.at(step, 1))
                pe.sem_inc(waits_apart, 1)
                pe.reg_load(odd[step.slot], odd_graph[0:1, step.slot:step.slot + 1])
                with pe.If(odd[step.slot]):
                    sum_odd(step)
                with pe.Else():
                    sum_plain(step)

            def end_sums(step):
                with pe.If(odd[step.slot]):
                    pe.wait_ge(pe_abs_used.sem, pe_abs_used.at(step, T))
                    pe.sem_inc(pe_sums.sem, 1)
                with pe.Else():
                    pe.wait_ge(act_rows.sem, act_rows.at(step, 2))
                    for t in range(T):
                        last = nc.tensor.matmul(sums_ps[:, t, :], sums_row[:, t * P:(t + 1) * P],
                                                ones[0:1, :].bitcast(F32), start=True, stop=True)
                    last.then_inc(pe_sums.sem, 1)

            def through_weights(step, t):
                first = FIRST_MATRIX[step.layer]
                width = 2 if step.gated else 1
                banks = len(x_banks(step))
                if t % 2 == 0:
                    pe.wait_ge(dve_xt.sem, dve_xt.at(step, t // 2 + 1))
                if t >= banks:
                    pe.wait_ge(dve_f.sem, dve_f.at(step, t - banks + 1))
                elif t == 0 and step.before():
                    pe.wait_ge(dve_f.sem, dve_f.at(step.before(), T))
                elif t == banks - 1 and step.before():
                    pe.wait_ge(dve_last.sem, dve_last.at(step.before(), T - 1 if step.gated else T))
                tile = slice(t * P, (t + 1) * P)
                parts = [(x_part, w_part, k) for k in range(K)
                         for x_part, w_part in ((xt_hi, w_hi), (xt_hi, w_lo), (xt_lo, w_hi))]
                for n, (x_part, w_part, k) in enumerate(parts):
                    last = nc.tensor.matmul(x_bank(step, t)[:, 0:width * D], x_part[:, k, tile],
                                            w_part[:, k, first:first + width, :],
                                            start=n == 0, stop=n == len(parts) - 1)
                last.then_inc(pe_x.sem, 1)
                if step.gated:
                    if t >= 2:
                        pe.wait_ge(dve_logit.sem, dve_logit.at(step, t - 1))
                    elif t == 1 and step.before():
                        pe.wait_ge(dve_last.sem, dve_last.at(step.before(), T))
                    for n, (x_part, w_part, k) in enumerate(parts):
                        last = nc.tensor.matmul(logit_bank(step, t), x_part[:, k, tile], w_part[:, k, first + 2, :],
                                                start=n == 0, stop=n == len(parts) - 1)
                    last.then_inc(pe_logit.sem, 1)

            def bank_free(step, stage, t):
                n = stage * T + t - PRODUCT_BANKS
                if stage == 0 and t == 1 and step.gated:
                    last_there = max(x_tile for x_tile in range(T) if x_bank(step, x_tile) is idle_bank(step, 1))
                    pe.wait_ge(dve_f.sem, dve_f.at(step, last_there + 1))
                    return
                if stage == 0 and t == 2:
                    if step.gated:
                        pe.wait_ge(dve_logit.sem, dve_logit.at(step, T))
                    return
                if n < 0:
                    step = step.before()
                    if step is None:
                        return
                    n += step.last_stage * T + T
                if n < step.last_stage * T:
                    pe.wait_ge(dve_link.sem, dve_link.at(step, n + 1))
                else:
                    pe.wait_ge(dve_last.sem, dve_last.at(step, n - step.last_stage * T + 1))

            def product(step, stage, general):
                blocks = [(m, t) for m in range(T) for t in (0, 1)]
                blocks += [(m, t) for t in range(2, T) for m in range(T)]
                after = step.after()
                for m, t in blocks:
                    if m == 0:
                        bank_free(step, stage, t)
                        if t == FLAG_TILE and stage == step.last_stage and after and after.layer == 0:
                            add_marks(after)
                    if t == 0:
                        pe.wait_ge(dve_f.sem, dve_f.at(step, stage * T + m + 1))
                    for part in (f_hi, f_lo):
                        f = part[:, f_buffer(step, stage), m, :]
                        block = adj[step.slot][:, m, t * P:(t + 1) * P]
                        if general:
                            block, f = block.bitcast(F32), f.bitcast(F32)
                        last = nc.tensor.matmul(product_bank(step, stage, t), block, f,
                                                start=(m == 0 and part is f_hi),
                                                stop=(m == T - 1 and part is f_lo))
                    if m == T - 1:
                        last.then_inc(pe_product.sem, 1)
                        if stage == step.last_stage and 3 <= t < 3 + PAIRS and next_turned(step):
                            turn(next_turned(step), t - 3)

            def one_round(rnd):
                for step in steps_of(rnd):
                    for t in range(T):
                        if step.apart and t % 4 == 0:
                            turn(step, t // 2)
                            turn(step, t // 2 + 1)
                        if step.before() or t >= X_AHEAD:
                            through_weights(step, t)
                        if step.layer == 0 and t == 0:
                            end_sums(step)
                    for stage in range(step.last_stage + 1):
                        with pe.If(odd[step.slot]):
                            product(step, stage, True)
                        with pe.Else():
                            product(step, stage, False)
                    if step.after() and step.after().layer == 0:
                        start_sums(step.after())

            pe.wait_ge(identity_steps, 2)
            for u in range(PAIRS):
                turn(steps_of(0)[0], u)
            pe.wait_ge(ones_set, 1)
            pe.wait_ge(w_lo_made, MATRICES)
            for t in range(X_AHEAD):
                through_weights(steps_of(0)[0], t)
            add_marks(steps_of(0)[0])
            start_sums(steps_of(0)[0])
            all_rounds(pe, one_round)

        @block.scalar
        def _(act):
            def store(step):
                act.wait_ge(act_x.sem, act_x.at(step, PAIRS))
                act.sem_inc(waits_apart, 1)
                act.dma_start(out_dram[graph_round(step), step.slot], xs[step.slot][:, :, :]).then_inc(stored[step.slot], 16)

            def load_next(step):
                at = graph_round(step)
                if isinstance(at, int) and at + 1 == ROUNDS:
                    return
                act.wait_ge(stored[step.slot], at * 16 + 16)
                act.sem_inc(waits_apart, 1)
                act.dma_start(xs[step.slot][:, :, :], x_dram[at + 1, step.slot]).then_inc(load_x[step.slot], 16)

            def turned(step, u):
                act.wait_ge(pe_turned.sem, pe_turned.at(step, u + 1))
                nc.scalar.activation(xt_hi[:, :, 2 * u * P:(2 * u + 2) * P], turn_ps[u % 2][:, :, :],
                                     ACT.Copy).then_inc(act_xt_hi.sem, 1)

            def mark(step, m):
                act.wait_ge(dve_masked.sem, dve_masked.at(step, m + 1))
                nc.scalar.activation(abs_adj[:, :], masked, ACT.Abs,
                                     accum_out=marks[:, m:m + 1]).then_inc(act_mark.sem, 1)

            def help_sums(step):
                act.wait_ge(dve_flag.sem, dve_flag.at(step, 1))
                act.sem_inc(waits_apart, 1)
                odd = act.value_load(odd_graph[0:1, step.slot:step.slot + 1])
                with act.If(odd):
                    for m in range(T):
                        if m:
                            act.wait_ge(pe_abs_used.sem, pe_abs_used.at(step, m))
                        nc.scalar.activation(abs_adj[:, :], adj[step.slot][:, m, :].bitcast(F32),
                                             ACT.Abs).then_inc(act_abs.sem, 1)
                    act.sem_inc(act_rows.sem, 2)
                with act.Else():
                    for h in range(2):
                        act.wait_ge(pe_rows.sem, pe_rows.at(step, h + 1))
                        nc.scalar.activation(sums_row[:, h * HALF:(h + 1) * HALF], rows_ps[h][0:1, :],
                                             ACT.Copy).then_inc(act_rows.sem, 1)
                    act.sem_inc(act_abs.sem, T)

            def tanh(step, t):
                act.wait_ge(dve_logit.sem, dve_logit.at(step, t + 1))
                nc.scalar.activation(gate[:, t, :], gate[:, t, :], ACT.Tanh, scale=0.5).then_inc(act_gate.sem, 1)

            def exponential(step, u):
                act.wait_ge(pool_mix.sem, pool_mix.at(step, u + 1))
                nc.scalar.activation(expo[:, u % 2], mixed[:, u % 2], ACT.Relu, scale=-1.0).then_inc(act_relu.sem, 1)
                act.wait_ge(act_relu.sem, act_relu.at(step, u + 1))
                nc.scalar.activation(expo[:, u % 2], expo[:, u % 2], ACT.Exp, scale=-1.0).then_inc(act_exp.sem, 1)

            def normalise(step, u):
                for t in (2 * u, 2 * u + 1):
                    act.wait_ge(pool_shift.sem, pool_shift.at(step, u + 1))
                    last = nc.scalar.activation(xs[step.slot][:, t, :], y_buffer(step, u)[:, t % 2, :], ACT.Identity,
                                                scale=rstd[:, t:t + 1], bias=shift[:, t:t + 1])
                last.then_inc(act_x.sem, 1)

            def one_round(rnd):
                for step in steps_of(rnd):
                    before = step.before()
                    for t in range(T):
                        if step.apart and t % 4 == 0:
                            if t:
                                normalise(before, 2)
                                normalise(before, 3)
                            else:
                                normalise(before, 1)
                            turned(step, t // 2)
                            turned(step, t // 2 + 1)
                        if step.apart and t == 2:
                            exponential(before, PAIRS - 1)
                        act.wait_ge(pe_x.sem, pe_x.at(step, t + 1))
                        if step.gated:
                            if before is not None and t % 2 == 0:
                                if before.gated:
                                    act.wait_ge(pool_mix.sem, pool_mix.at(before, t // 2 + 1))
                                elif before.layer == CHAIN:
                                    act.wait_ge(dve_act.sem, dve_act.at(before, t // 2 + 1))
                                else:
                                    act.wait_ge(dve_last.sem, dve_last.at(before, t + 2))
                            nc.scalar.activation(side[:, t, :], x_bank(step, t)[:, D:2 * D], ACT.Copy)
                        if step.layer == 0 and t % (T // 2) == 0:
                            act.wait_ge(pool_norm.sem, pool_norm.at(step, 1 + t // (T // 2)))
                        nc.scalar.activation(f_hi[:, f_buffer(step, 0), t, :], x_bank(step, t)[:, 0:D], ACT.Copy,
                                             scale=norm_of(step, t) if step.gated else 1.0).then_inc(act_f_hi.sem, 1)
                        if step.gated and t >= 1:
                            tanh(step, t - 1)
                        if before is not None and not step.apart:
                            if before.gated and t == (1 if step.gated else 5):
                                exponential(before, PAIRS - 1)
                            if step.gated and t in normalise_places(step):
                                normalise(before, 1 + normalise_places(step).index(t))
                        if before is not None and before.layer == LAST and before.slot == 0 and t == 4:
                            store(before)
                        if marked_at(step, -1, t) is not None:
                            mark(step.after(), marked_at(step, -1, t))
                    if step.gated:
                        tanh(step, T - 1)
                    if before is not None and before.layer == LAST and before.slot == 0:
                        load_next(before)
                    if before is not None and not step.gated and not step.apart:
                        normalise(before, 1)
                        if step.layer == LAST:
                            normalise(before, 2)
                    for stage in range(step.last_stage + 1):
                        for t in range(T):
                            if before is not None and not step.gated and not step.apart and stage == 0:
                                if step.layer == CHAIN and t in (2, 4):
                                    normalise(before, 1 + t // 2)
                                if step.layer == LAST and t == 1:
                                    normalise(before, 3)
                            if stage < step.last_stage:
                                act.wait_ge(pe_product.sem, pe_product.at(step, stage * T + t + 1))
                                nc.scalar.activation(f_hi[:, f_buffer(step, stage + 1), t, :], product_bank(step, stage, t),
                                                     ACT.Copy, scale=norms[:, step.slot, INV_SUM, t:t + 1]
                                                     ).then_inc(act_f_hi.sem, 1)
                                if before is not None and before.layer == LAST and before.slot == 1:
                                    if (stage, t) == (0, 5):
                                        store(before)
                                    if (stage, t) == (1, 1):
                                        load_next(before)
                            else:
                                if t == (5 if step.layer == LAST else 7):
                                    normalise(step, 0)
                                if next_turned(step) and 3 <= t < 3 + PAIRS:
                                    turned(next_turned(step), t - 3)
                                if step.gated and t in (3, 5, 7):
                                    exponential(step, t // 2 - 1)
                            if marked_at(step, stage, t) is not None:
                                mark(step.after(), marked_at(step, stage, t))
                    if step.after() and step.after().layer == 0:
                        help_sums(step.after())

            act.dma_start(xs[0][:, :, :], x_dram[0, 0]).then_inc(load_x[0], 16)
            for j, w in enumerate((theta0, wh0, wt0, w1t, theta2, wh2, wt2, w3)):
                act.dma_start(weight_f32[j // 4][:, j % 4], w.rearrange("(k p) d -> p k d", p=P)).then_inc(load_w, 16)
            for j, b in enumerate((bt0, bt2)):
                act.dma_start(gate_bias[:, j, :], b.partition_broadcast(P)).then_inc(load_w, 16)
            act.dma_start(last_bias[:, :], bias3.partition_broadcast(P)).then_inc(load_w, 16)
            act.dma_start(taps[:, 0:TAPS], conv_w.partition_broadcast(P)).then_inc(load_w, 16)
            act.dma_start(taps[:, TAPS:TAPS + 1], conv_b.partition_broadcast(P)).then_inc(load_w, 16)
            for u in range(PAIRS):
                turned(steps_of(0)[0], u)
            act.wait_ge(load_w, 16 * (MATRICES + 5))
            for j in range(MATRICES):
                nc.scalar.activation(w_hi[:, :, j, :], weight_f32[j // 4][:, j % 4], ACT.Copy).then_inc(w_hi_made, 1)
            act.wait_ge(w_lo_made, MATRICES)
            for m in range(T):
                mark(steps_of(0)[0], m)
            act.dma_start(xs[1][:, :, :], x_dram[0, 1]).then_inc(load_x[1], 16)
            help_sums(steps_of(0)[0])
            all_rounds(act, one_round)
            end = steps_of(ROUNDS - 1)[-1]
            for u in range(1, PAIRS):
                normalise(end, u)
                if u >= 2:
                    tiles = slice(0, T - 2) if u == 2 else slice(T - 2, T)
                    act.wait_ge(act_x.sem, act_x.at(end, u + 1))
                    act.dma_start(out_dram[graph_round(end), end.slot][:, tiles, :],
                                  xs[end.slot][:, tiles, :]).then_inc(stored[end.slot], 16)
            act.wait_ge(stored[0], ROUNDS * 16)
            act.wait_ge(stored[1], (ROUNDS + 1) * 16)

        @block.vector
        def _(dve):
            def mask(step, part):
                h = 2 * part
                for half in (h, h + 1):
                    dve.wait_ge(moved[half % STAGES], moves(graph_round(step), step.slot, half))
                if part:
                    dve.wait_ge(act_mark.sem, act_mark.at(step, part))
                nc.vector.tensor_scalar(masked.rearrange("p (m n) -> p m n", m=2),
                                        adj[step.slot][:, h % T:h % T + 2, columns(h)].bitcast(I32),
                                        SIGN_OR_LOW_BITS, None, ALU.bitwise_and).then_inc(dve_masked.sem, 1)

            def find_flag(step):
                dve.wait_ge(pe_marks.sem, pe_marks.at(step, 1))
                nc.vector.tensor_reduce(most[:, :], marks_ps, AX.X, ALU.max).then_inc(dve_most.sem, 1)
                dve.wait_ge(dve_most.sem, dve_most.at(step, 1))
                nc.vector.tensor_scalar(odd_graph[0:1, step.slot:step.slot + 1], most[:, :], 0.0, None,
                                        ALU.not_equal).then_inc(dve_flag.sem, 1)

            def take_sums(step):
                s = step.slot
                dve.wait_ge(pe_sums.sem, pe_sums.at(step, 1))
                nc.vector.tensor_copy(sums[:, s], sums_ps).then_inc(dve_sums.sem, 1)
                dve.wait_ge(dve_sums.sem, dve_sums.at(step, 1))
                nc.vector.tensor_scalar(norms[:, s, INV_SUM, :], sums[:, s, :, 1], ROW_SUM_EPS, None,
                                        ALU.add).then_inc(dve_shifted.sem, 1)

            def invert_sums(step):
                s = step.slot
                dve.wait_ge(dve_shifted.sem, dve_shifted.at(step, 1))
                nc.vector.reciprocal(norms[:, s, INV_SUM, :], norms[:, s, INV_SUM, :]).then_inc(dve_inv.sem, 1)
                dve.wait_ge(dve_inv.sem, dve_inv.at(step, 1))
                for k in range(1, TAPS):
                    nc.vector.tensor_scalar(norms[:, s, CONV + k, :], norms[:, s, INV_SUM, :],
                                            taps[:, k:k + 1], None, ALU.mult)

            def turned(step, u):
                dve.wait_ge(act_xt_hi.sem, act_xt_hi.at(step, u + 1))
                at = slice(2 * u * P, (2 * u + 2) * P)
                nc.vector.tensor_tensor(xt_lo[:, :, at], turn_ps[u % 2][:, :, :], xt_hi[:, :, at].bitcast(F32),
                                        ALU.subtract).then_inc(dve_xt.sem, 1)

            def logits(step, t):
                dve.wait_ge(pe_logit.sem, pe_logit.at(step, t + 1))
                if t % 2 == 0 and step.gated_before():
                    dve.wait_ge(pool_mix.sem, pool_mix.at(step.gated_before(), t // 2 + 1))
                nc.vector.tensor_tensor(gate[:, t, :], logit_bank(step, t), gate_bias[:, GATED.index(step.layer), :],
                                        ALU.add).then_inc(dve_logit.sem, 1)

            def remainder(step, stage, t, source, scale):
                dve.wait_ge(act_f_hi.sem, act_f_hi.at(step, stage * T + t + 1))
                b = f_buffer(step, stage)
                nc.vector.scalar_tensor_tensor(f_lo[:, b, t, :], source, scale, f_hi[:, b, t, :].bitcast(F32),
                                               ALU.mult, ALU.subtract).then_inc(dve_f.sem, 1)

            def chain_link(step, stage, t):
                s = step.slot
                source = product_bank(step, stage, t)
                dve.wait_ge(pe_product.sem, pe_product.at(step, stage * T + t + 1))
                if stage < step.last_stage:
                    remainder(step, stage + 1, t, source, norms[:, s, INV_SUM, t:t + 1])
                if stage == 0 and t % 2 == 0:
                    dve.wait_ge(pool_side.sem, pool_side.at(step, t // 2 + 1))
                added = dve_link if stage < step.last_stage else dve_last
                nc.vector.scalar_tensor_tensor(side[:, t, :], source, norms[:, s, CONV + stage + 1, t:t + 1],
                                               side[:, t, :], ALU.mult, ALU.add).then_inc(added.sem, 1)

            def read_last(step, t):
                source = product_bank(step, step.last_stage, t)
                u = t // 2
                if step.layer == CHAIN:
                    chain_link(step, step.last_stage, t)
                    return
                dve.wait_ge(pe_product.sem, pe_product.at(step, t + 1))
                if step.layer == LAST:
                    if t % 2 == 0:
                        dve.wait_ge(pool_side.sem, pool_side.at(step, u + 1))
                        if u < PAIRS - 1:
                            dve.wait_ge(act_x.sem, act_x.at(step.before(), u + 2))
                        else:
                            dve.wait_ge(act_x.sem, act_x.at(step, 1))
                    nc.vector.tensor_tensor(y_buffer(step, u)[:, t % 2, :], source, side[:, t, :],
                                            ALU.add).then_inc(dve_last.sem, 1)
                    return
                nc.vector.scalar_tensor_tensor(mixed[:, u % 2, t % 2, :], source, norm_of(step, t),
                                               side[:, t, :], ALU.mult, ALU.subtract).then_inc(dve_last.sem, 1)

            def residual(step, u):
                to = y_buffer(step, u)
                x_pair = pair(xs[step.slot], u)
                if step.layer != LAST:
                    if u == 0 and step.before():
                        dve.wait_ge(act_x.sem, act_x.at(step.before(), PAIRS))
                    elif u == PAIRS - 1:
                        dve.wait_ge(act_x.sem, act_x.at(step, 1))
                if step.gated:
                    dve.wait_ge(pool_mix.sem, pool_mix.at(step, u + 1))
                    nc.vector.scalar_tensor_tensor(to, mixed[:, u % 2], 0.0, x_pair, ALU.max,
                                                   ALU.add).then_inc(dve_act.sem, 1)
                    dve.wait_ge(dve_act.sem, dve_act.at(step, u + 1))
                    dve.wait_ge(act_exp.sem, act_exp.at(step, u + 1))
                    nc.vector.scalar_tensor_tensor(to, expo[:, u % 2], -1.0, to, ALU.add,
                                                   ALU.add).then_inc(dve_y.sem, 1)
                elif step.layer == CHAIN:
                    dve.wait_ge(dve_last.sem, dve_last.at(step, 2 * u + 2))
                    nc.vector.scalar_tensor_tensor(to, pair(side, u), LEAKY_SLOPE, pair(side, u), ALU.mult,
                                                   ALU.max).then_inc(dve_act.sem, 1)
                    dve.wait_ge(dve_act.sem, dve_act.at(step, u + 1))
                    nc.vector.tensor_tensor(to, to, x_pair, ALU.add).then_inc(dve_y.sem, 1)
                if step.layer == LAST:
                    dve.wait_ge(dve_last.sem, dve_last.at(step, 2 * u + 2))
                else:
                    dve.wait_ge(dve_y.sem, dve_y.at(step, u + 1))
                if u:
                    dve.wait_ge(dve_mean.sem, dve_mean.at(step, u))
                elif step.before():
                    dve.wait_ge(dve_mean.sem, dve_mean.at(step.before(), PAIRS))
                for j in range(2):
                    last = nc.vector.bn_stats(stats[:, j, :], to[:, j, :])
                last.then_inc(dve_stats.sem, 1)
                dve.wait_ge(dve_stats.sem, dve_stats.at(step, u + 1))
                dve.sem_inc(waits_apart, 1)
                for j in range(2):
                    last = nc.vector.bn_aggr(mean_var[:, 2 * u + j, :], stats[:, j, :])
                last.then_inc(dve_mean.sem, 1)

            def one_round(rnd):
                for step in steps_of(rnd):
                    before = step.before()
                    for t in range(T):
                        if step.apart and t % 4 == 0:
                            residual(before, 2 + t // 4)
                            turned(step, t // 2)
                            turned(step, t // 2 + 1)
                        if step.gated:
                            logits(step, t)
                        else:
                            dve.wait_ge(pe_x.sem, pe_x.at(step, t + 1))
                        if step.layer == 0 and t == 0:
                            take_sums(step)
                        remainder(step, 0, t, x_bank(step, t)[:, 0:D], norm_of(step, t) if step.gated else 1.0)
                        if step.layer == 0 and t == 0:
                            invert_sums(step)
                        if before is not None and not step.apart and t in residual_places(step):
                            residual(before, 2 + residual_places(step).index(t))
                        if looked_at(step, -1, t) is not None:
                            mask(step.after(), looked_at(step, -1, t))
                    for stage in range(step.last_stage + 1):
                        for t in range(T):
                            if stage < step.last_stage:
                                chain_link(step, stage, t)
                            else:
                                read_last(step, t)
                            if stage == step.last_stage:
                                if next_turned(step) and 3 <= t < 3 + PAIRS:
                                    turned(next_turned(step), t - 3)
                                if t == FLAG_TILE - 1 and step.after() and step.after().layer == 0:
                                    find_flag(step.after())
                                if t in (3, 5):
                                    residual(step, t // 2 - 1)
                            if looked_at(step, stage, t) is not None:
                                mask(step.after(), looked_at(step, stage, t))

            nc.vector.memset(ones[:, :].bitcast(F32), 1.0).then_inc(ones_set, 1)
            for u in range(PAIRS):
                turned(steps_of(0)[0], u)
            dve.wait_ge(load_w, 16 * (MATRICES + 5))
            for j in range(MATRICES):
                dve.wait_ge(w_hi_made, j + 1)
                nc.vector.tensor_tensor(w_lo[:, :, j, :], weight_f32[j // 4][:, j % 4],
                                        w_hi[:, :, j, :].bitcast(F32), ALU.subtract).then_inc(w_lo_made, 1)
            for m in range(T):
                mask(steps_of(0)[0], m)
            find_flag(steps_of(0)[0])
            all_rounds(dve, one_round)
            end = steps_of(ROUNDS - 1)[-1]
            residual(end, 2)
            residual(end, 3)

        @block.gpsimd
        def _(pool):
            def find_norms(step):
                s = step.slot
                pool.wait_ge(dve_sums.sem, dve_sums.at(step, 1))
                pool.sem_inc(waits_apart, 1)
                parts = ((ABS_NORM, 0, slice(0, T // 2)), (ABS_NORM, 0, slice(T // 2, T)), (NORM, 1, slice(0, T)))
                for n, (row, j, tiles) in enumerate(parts):
                    nc.gpsimd.tensor_scalar(norms[:, s, row, tiles], sums[:, s, tiles, j], DEGREE_EPS, None,
                                            ALU.add).then_inc(pool_shifted.sem, 1)
                    pool.wait_ge(pool_shifted.sem, pool_shifted.at(step, n + 1))
                    nc.gpsimd.tensor_tensor(norms[:, s, row, tiles], norms[:, s, row, tiles], minus_half[:, tiles],
                                            ALU.pow).then_inc(pool_norm.sem, 1)

            def gates(step, u):
                pool.wait_ge(act_gate.sem, act_gate.at(step, 2 * u + 2))
                pool.sem_inc(waits_apart, 1)
                nc.gpsimd.tensor_scalar(pair(gate, u), pair(gate, u), 0.5, 0.5, ALU.mult,
                                        ALU.add).then_inc(pool_gate.sem, 1)

            def mix(step, u):
                pool.wait_ge(dve_last.sem, dve_last.at(step, 2 * u + 2))
                pool.wait_ge(pool_gate.sem, pool_gate.at(step, u + 1))
                nc.gpsimd.tensor_tensor(mixed[:, u % 2], mixed[:, u % 2], pair(gate, u),
                                        ALU.mult).then_inc(pool_mul.sem, 1)
                pool.wait_ge(pool_mul.sem, pool_mul.at(step, u + 1))
                nc.gpsimd.tensor_tensor(mixed[:, u % 2], mixed[:, u % 2], pair(side, u), ALU.add).then_inc(pool_mix.sem, 1)

            def inverse_deviation(step, u):
                pool.wait_ge(dve_mean.sem, dve_mean.at(step, u + 1))
                pool.sem_inc(waits_apart, 1)
                at = rstd[:, 2 * u:2 * u + 2]
                nc.gpsimd.tensor_scalar(at, mean_var[:, 2 * u:2 * u + 2, 1], LN_EPS, None, ALU.add)
                nc.gpsimd.tensor_scalar(shift[:, 2 * u:2 * u + 2], mean_var[:, 2 * u:2 * u + 2, 0], -1.0, None,
                                        ALU.mult).then_inc(pool_var.sem, 1)
                pool.wait_ge(pool_var.sem, pool_var.at(step, u + 1))
                nc.gpsimd.tensor_tensor(at, at, minus_half[:, 0:2], ALU.pow).then_inc(pool_rstd.sem, 1)
                pool.wait_ge(pool_rstd.sem, pool_rstd.at(step, u + 1))
                nc.gpsimd.tensor_tensor(shift[:, 2 * u:2 * u + 2], shift[:, 2 * u:2 * u + 2], at,
                                        ALU.mult).then_inc(pool_shift.sem, 1)

            def side_free(step, u):
                before = step.before()
                if before.gated:
                    pool.wait_ge(pool_mix.sem, pool_mix.at(before, u + 1))
                elif before.layer == CHAIN:
                    pool.wait_ge(dve_act.sem, dve_act.at(before, u + 1))
                else:
                    pool.wait_ge(dve_last.sem, dve_last.at(before, 2 * u + 2))

            def first_term(step, u):
                pool.wait_ge(dve_f.sem, dve_f.at(step, 2 * u + 2))
                side_free(step, u)
                b = f_buffer(step, 0)
                nc.gpsimd.tensor_tensor(pair(side, u), pair(f_hi[:, b].bitcast(F32), u), pair(f_lo[:, b].bitcast(F32), u),
                                        ALU.add).then_inc(pool_h.sem, 1)
                pool.wait_ge(pool_h.sem, pool_h.at(step, u + 1))
                pool.sem_inc(waits_apart, 1)
                nc.gpsimd.tensor_scalar(pair(side, u), pair(side, u), taps[:, 0:1], taps[:, TAPS:TAPS + 1], ALU.mult,
                                        ALU.add).then_inc(pool_side.sem, 1)

            def biased(step, u):
                pool.wait_ge(act_x.sem, act_x.at(step.layer_before(), u + 1))
                side_free(step, u)
                for t in (2 * u, 2 * u + 1):
                    last = nc.gpsimd.tensor_tensor(side[:, t, :], xs[step.slot][:, t, :], last_bias[:, :], ALU.add)
                last.then_inc(pool_side.sem, 1)

            def one_round(rnd):
                for step in steps_of(rnd):
                    before = step.before()
                    if before is not None and before.gated:
                        mix(before, PAIRS - 1)
                    if step.layer == 0:
                        find_norms(step)
                    if before is not None and (step.gated or step.apart):
                        inverse_deviation(before, 2)
                    if step.apart:
                        inverse_deviation(before, 3)
                    for u in range(PAIRS):
                        if step.layer == LAST:
                            biased(step, u)
                        if step.layer == CHAIN:
                            first_term(step, u)
                        if step.gated:
                            gates(step, u)
                        elif not step.apart and u in (1, 3):
                            inverse_deviation(before, 2 + u // 2)
                        if before is not None and step.gated and u == 0:
                            inverse_deviation(before, 3)
                    if step.gated:
                        mix(step, 0)
                        mix(step, 1)
                    inverse_deviation(step, 0)
                    if step.gated:
                        mix(step, 2)
                    inverse_deviation(step, 1)

            nc.gpsimd.memset(identity[:, :], 0.0).then_inc(identity_steps, 1)
            pool.wait_ge(identity_steps, 1)
            nc.gpsimd.affine_select(out=identity[:, :], in_=identity[:, :], compare_op=ALU.not_equal, fill=1.0,
                                    base=0, pattern=[[-1, P]], channel_multiplier=1).then_inc(identity_steps, 1)
            nc.gpsimd.memset(minus_half[:, :], -0.5).then_inc(half_set, 1)
            pool.wait_ge(half_set, 1)
            pool.wait_ge(load_w, 16 * (MATRICES + 5))
            all_rounds(pool, one_round)
            end = steps_of(ROUNDS - 1)[-1]
            inverse_deviation(end, 2)
            inverse_deviation(end, 3)


INPUTS = ["x", "adj", "L0_gnn_theta", "L0_gnn_W_h", "L0_gnn_W_t", "L0_gnn_b_t", "L1_gnn_W", "L1_gnn_conv_w",
          "L1_gnn_conv_b", "L2_gnn_W_t", "L2_gnn_b_t", "L2_gnn_W_h", "L2_gnn_theta", "L3_gnn_weight", "L3_gnn_bias"]
TRANSPOSED = {"adj": (0, 2, 1), "L1_gnn_W": (1, 0)}


def kernel(**inputs):
    import numpy as np
    import concourse.bacc as bacc
    from concourse.bass_utils import run_bass_kernel_spmd

    nc = bacc.Bacc("TRN2", target_bir_lowering=False, num_devices=1)
    arrays, args = {}, []
    for name in INPUTS:
        a = np.asarray(inputs[name])
        a = np.ascontiguousarray(a.transpose(TRANSPOSED[name]) if name in TRANSPOSED else a)
        arrays[f"in_{name}"] = a
        args.append(nc.dram_tensor(f"in_{name}", a.shape, mybir.dt.from_np(a.dtype), kind="ExternalInput").ap())
    shape = arrays["in_x"].shape
    args.append(nc.dram_tensor("out", shape, F32, kind="ExternalOutput").ap())
    gnn_stack(nc, *args)
    result = run_bass_kernel_spmd(nc, [arrays], core_ids=[0])
    return result.results[0]["out"]
```
